# Optimizing a Trainium2 kernel written in Bass

```python
import numpy as np
import jax
import jax.numpy as jnp

def _softmax(x, axis=-1):
    return jax.nn.softmax(x, axis=axis)

def _gelu(x):
    return jax.nn.gelu(x, approximate=True)

def _silu(x):
    return jax.nn.silu(x)

def _sigmoid(x):
    return jax.nn.sigmoid(x)

def _layernorm(x, axis=-1, eps=1e-05):
    m = jnp.mean(x, axis=axis, keepdims=True)
    v = jnp.var(x, axis=axis, keepdims=True)
    return (x - m) / jnp.sqrt(v + eps)

def _scatter_add(tgt, idx, src, axis=0):
    return tgt.at[idx].add(src)

def _segment_sum(src, seg, n):
    return jax.ops.segment_sum(src, seg, n)
kernel_name = 'mk_sandwich_d1_jaxref_r8_95c36d'

def setup_inputs(seed: int=0):
    np.random.seed(seed)
    _w = jnp.asarray

    def _L0_attn_setup():
        import jax, jax.numpy as jnp
        import numpy as np
        B, T, D = (1, 512, 128)
        H, KD, VD = (16, 64, 64)
        MIN_THETA, MAX_THETA = (1.0, 10000.0)

        def _sin_cos(t, d, dtype):
            half = d // 2
            p = jnp.arange(half, dtype=dtype) / (half - 1)
            thetas = MIN_THETA * (MAX_THETA / MIN_THETA) ** p
            pos = jnp.arange(t, dtype=dtype)[:, None] / thetas[None, :]
            return (jnp.sin(pos), jnp.cos(pos))

        def _rope(x, sin, cos):
            d = x.shape[-1] // 2
            x_hi, x_lo = (x[..., :d], x[..., d:])
            y_lo = x_lo * cos + x_hi * sin
            y_hi = x_hi * cos - x_lo * sin
            return jnp.concatenate([y_lo, y_hi], axis=-1)
        key = jax.random.key(seed)
        k0, k1, k2 = jax.random.split(key, 3)
        x = jax.random.normal(k0, (B, T, D), dtype=jnp.float32)
        W_in = jax.random.normal(k1, ((2 * KD + VD) * H, D), dtype=jnp.float32) * 0.02
        b_in = jnp.zeros(((2 * KD + VD) * H,), dtype=jnp.float32)
        W_out = jax.random.normal(k2, (D, H * VD), dtype=jnp.float32) * 0.02
        b_out = jnp.zeros((D,), dtype=jnp.float32)
        return {'x': x, 'W_in': W_in, 'b_in': b_in, 'W_out': W_out, 'b_out': b_out}
    _L0_attn_in = _L0_attn_setup()

    def _L0_ffn_setup():
        import jax, jax.numpy as jnp
        import numpy as np
        S, B, H = (256, 1, 128)
        N_HEADS = 16
        HEAD_DIM = H // N_HEADS
        E, K, F = (8, 2, 256)
        EPS = 1e-05

        def layernorm(x, w, b):
            mu = jnp.mean(x, axis=-1, keepdims=True)
            var = jnp.mean(jnp.square(x - mu), axis=-1, keepdims=True)
            return (x - mu) * jax.lax.rsqrt(var + EPS) * w + b
        key = jax.random.key(seed)
        ks = jax.random.split(key, 8)
        std = 0.02
        return {'x': jax.random.normal(ks[0], (S, B, H), dtype=jnp.float32), 'ln1_w': jnp.ones((H,), jnp.float32), 'ln1_b': jnp.zeros((H,), jnp.float32), 'in_proj_w': jax.random.normal(ks[1], (3 * H, H), jnp.float32) * std, 'in_proj_b': jnp.zeros((3 * H,), jnp.float32), 'out_proj_w': jax.random.normal(ks[2], (H, H), jnp.float32) * std, 'out_proj_b': jnp.zeros((H,), jnp.float32), 'ln2_w': jnp.ones((H,), jnp.float32), 'ln2_b': jnp.zeros((H,), jnp.float32), 'router_w': jax.random.normal(ks[3], (E, H), jnp.float32) * std, 'w1': jax.random.normal(ks[4], (E, H, F), jnp.float32) * std, 'w2': jax.random.normal(ks[5], (E, F, H), jnp.float32) * std}
    _L0_ffn_in = _L0_ffn_setup()
    _d = {'L0_attn_x': _L0_attn_in['x'], 'L0_attn_W_in': _L0_attn_in['W_in'], 'L0_attn_b_in': _L0_attn_in['b_in'], 'L0_attn_W_out': _L0_attn_in['W_out'], 'L0_attn_b_out': _L0_attn_in['b_out'], 'L0_ffn_ln1_w': _L0_ffn_in['ln1_w'], 'L0_ffn_ln1_b': _L0_ffn_in['ln1_b'], 'L0_ffn_in_proj_w': _L0_ffn_in['in_proj_w'], 'L0_ffn_in_proj_b': _L0_ffn_in['in_proj_b'], 'L0_ffn_out_proj_w': _L0_ffn_in['out_proj_w'], 'L0_ffn_out_proj_b': _L0_ffn_in['out_proj_b'], 'L0_ffn_ln2_w': _L0_ffn_in['ln2_w'], 'L0_ffn_ln2_b': _L0_ffn_in['ln2_b'], 'L0_ffn_router_w': _L0_ffn_in['router_w'], 'L0_ffn_w1': _L0_ffn_in['w1'], 'L0_ffn_w2': _L0_ffn_in['w2']}
    _x0 = _d['L0_attn_x']
    _d['L0_attn_x'] = jax.random.normal(jax.random.fold_in(jax.random.key(seed), 1), (32, 256, 128), dtype=_x0.dtype)
    del _x0
    return _d

def reference(L0_attn_x, L0_attn_W_in, L0_attn_b_in, L0_attn_W_out, L0_attn_b_out, L0_ffn_ln1_w, L0_ffn_ln1_b, L0_ffn_in_proj_w, L0_ffn_in_proj_b, L0_ffn_out_proj_w, L0_ffn_out_proj_b, L0_ffn_ln2_w, L0_ffn_ln2_b, L0_ffn_router_w, L0_ffn_w1, L0_ffn_w2):

    def _L0_attn_ref(x, W_in, b_in, W_out, b_out):
        import jax, jax.numpy as jnp
        import numpy as np
        B, T, D = (1, 512, 128)
        H, KD, VD = (16, 64, 64)
        MIN_THETA, MAX_THETA = (1.0, 10000.0)

        def _sin_cos(t, d, dtype):
            half = d // 2
            p = jnp.arange(half, dtype=dtype) / (half - 1)
            thetas = MIN_THETA * (MAX_THETA / MIN_THETA) ** p
            pos = jnp.arange(t, dtype=dtype)[:, None] / thetas[None, :]
            return (jnp.sin(pos), jnp.cos(pos))

        def _rope(x, sin, cos):
            d = x.shape[-1] // 2
            x_hi, x_lo = (x[..., :d], x[..., d:])
            y_lo = x_lo * cos + x_hi * sin
            y_hi = x_hi * cos - x_lo * sin
            return jnp.concatenate([y_lo, y_hi], axis=-1)
        b, t, _ = x.shape
        proj = x @ W_in.T + b_in
        i1, i2 = (KD * H, 2 * KD * H)
        q = proj[..., :i1].reshape(b, t, H, KD).transpose(0, 2, 1, 3)
        k = proj[..., i1:i2].reshape(b, t, H, KD).transpose(0, 2, 1, 3)
        v = proj[..., i2:].reshape(b, t, H, VD).transpose(0, 2, 1, 3)
        sin, cos = _sin_cos(t, KD, x.dtype)
        q = _rope(q, sin, cos)
        k = _rope(k, sin, cos)
        scale = 1.0 / np.sqrt(KD)
        att = jnp.einsum('bhqd,bhkd->bhqk', q, k) * jnp.asarray(scale, x.dtype)
        mask = jnp.tril(jnp.ones((t, t), dtype=bool))
        att = jnp.where(mask[None, None], att, jnp.asarray(-jnp.inf, x.dtype))
        att = jax.nn.softmax(att, axis=-1)
        y = jnp.einsum('bhqk,bhkd->bhqd', att, v)
        y = y.transpose(0, 2, 1, 3).reshape(b, t, H * VD)
        return y @ W_out.T + b_out

    def _L0_ffn_ref(x, ln1_w, ln1_b, in_proj_w, in_proj_b, out_proj_w, out_proj_b, ln2_w, ln2_b, router_w, w1, w2):
        import jax, jax.numpy as jnp
        import numpy as np
        S, B, H = (256, 1, 128)
        N_HEADS = 16
        HEAD_DIM = H // N_HEADS
        E, K, F = (8, 2, 256)
        EPS = 1e-05

        def layernorm(x, w, b):
            mu = jnp.mean(x, axis=-1, keepdims=True)
            var = jnp.mean(jnp.square(x - mu), axis=-1, keepdims=True)
            return (x - mu) * jax.lax.rsqrt(var + EPS) * w + b
        s, b, h = x.shape
        hn = layernorm(x, ln1_w, ln1_b)
        qkv = hn @ in_proj_w.T + in_proj_b
        q, k, v = jnp.split(qkv, 3, axis=-1)
        q = q.reshape(s, b, N_HEADS, HEAD_DIM)
        k = k.reshape(s, b, N_HEADS, HEAD_DIM)
        v = v.reshape(s, b, N_HEADS, HEAD_DIM)
        scores = jnp.einsum('sbnd,tbnd->bnst', q, k) / np.sqrt(HEAD_DIM)
        causal = jnp.tril(jnp.ones((s, s), bool))
        scores = jnp.where(causal[None, None], scores, -jnp.inf)
        probs = jax.nn.softmax(scores, axis=-1)
        attn = jnp.einsum('bnst,tbnd->sbnd', probs, v).reshape(s, b, h)
        attn = attn @ out_proj_w.T + out_proj_b
        x1 = x + attn
        hn2 = layernorm(x1, ln2_w, ln2_b).reshape(s * b, h)
        logits = hn2 @ router_w.T
        rp = jax.nn.softmax(logits, axis=-1)
        topw, topi = jax.lax.top_k(rp, K)
        gates = jnp.sum(jax.nn.one_hot(topi, E, dtype=hn2.dtype) * topw[..., None], axis=1)
        hmid = jax.nn.gelu(jnp.einsum('th,ehf->tef', hn2, w1), approximate=False)
        y = jnp.einsum('tef,efh->th', hmid * gates[:, :, None], w2)
        return x1 + y.reshape(s, b, h)
    x = L0_attn_x
    x = x + _layernorm(_L0_attn_ref(_layernorm(x, axis=-1), L0_attn_W_in, L0_attn_b_in, L0_attn_W_out, L0_attn_b_out), axis=-1)
    x = x + _layernorm(_L0_ffn_ref(_layernorm(x, axis=-1), L0_ffn_ln1_w, L0_ffn_ln1_b, L0_ffn_in_proj_w, L0_ffn_in_proj_b, L0_ffn_out_proj_w, L0_ffn_out_proj_b, L0_ffn_ln2_w, L0_ffn_ln2_b, L0_ffn_router_w, L0_ffn_w1, L0_ffn_w2), axis=-1)
    return x

_drawn_inputs = setup_inputs


def setup_inputs(seed=0):
    import zlib

    import numpy as np

    out = dict(_drawn_inputs(seed))
    spreads = {'L0_attn_b_in': (0.0, 0.1),
     'L0_attn_b_out': (0.0, 0.1),
     'L0_ffn_ln1_w': (1.0, 0.6),
     'L0_ffn_ln1_b': (0.0, 0.8),
     'L0_ffn_in_proj_b': (0.0, 0.773),
     'L0_ffn_out_proj_b': (0.0, 0.1),
     'L0_ffn_ln2_w': (1.0, 0.6),
     'L0_ffn_ln2_b': (0.0, 0.8)}
    factors = {'L0_ffn_in_proj_w': 3.216,
     'L0_ffn_out_proj_w': 3.023,
     'L0_ffn_router_w': 8.0,
     'L0_ffn_w1': 8.0,
     'L0_ffn_w2': 8.0}
    for name, (base, spread) in spreads.items():
        noise = np.random.default_rng([zlib.crc32(name.encode()), seed]).standard_normal(out[name].shape)
        drawn = base * np.exp(spread * noise) if base else spread * noise
        out[name] = jnp.asarray(drawn.astype(out[name].dtype))
    for name, factor in factors.items():
        out[name] = (out[name] * factor).astype(out[name].dtype)
    return out
```

```python
from contextlib import ExitStack

import numpy as np

import concourse.bass as bass
from concourse import mybir

ALU = mybir.AluOpType
ACT = mybir.ActivationFunctionType
AXIS_X = mybir.AxisListType.X
F32 = mybir.dt.float32
F32R = mybir.dt.float32r
BF16 = mybir.dt.bfloat16

ROWS, COLS, D = 32, 256, 128
HEADS, HEAD_DIM = 16, 64
HALF = HEAD_DIM // 2
QUADS, PAIRS = HEADS // 4, HEADS // 2
FEATS = HEADS * HEAD_DIM
TILES = COLS // 128
EPS = 1e-5
MASKED = -1e30
MIN_THETA, MAX_THETA = 1.0, 10000.0

HEADS2, HD2 = 16, 8
EXPERTS, TOP, FF = 8, 2, 256
CC = 16
TOK, CHUNKS = CC * ROWS, COLS // CC
CT = TOK // 128

HI, LO = 0, 1
Q_SIDE, K_SIDE, K_SWAPPED = 0, 1, 2
STACK_DMAS = 32


class Row:

    def __init__(self, pair, k, total=ROWS):
        self.pair, self.k, self.total = pair, k, total
        self.parity = k % 2
        self.static = isinstance(pair, int)

    def __add__(self, n):
        return Row(self.pair, self.k + n, self.total)

    def number(self):
        return self.pair * 2 + self.k

    def exists(self):
        return not self.static or 0 <= self.number() < self.total

    def count(self, per_row, k):
        return self.pair * (2 * per_row) + (self.k * per_row + k)

    def count_of_parity(self, per_row, k):
        return self.pair * per_row + (self.k // 2 * per_row + k)


def wait(engine, semaphore, value):
    if isinstance(value, int) and value <= 0:
        return
    engine.wait_ge(semaphore, value)


def wait_apart(dve, semaphore, value, spacer):
    wait(dve, semaphore, value)
    if not isinstance(value, int):
        dve.memset(spacer, 0.0)


def attention_part(nc, x, w_qkv, w_out, bias_qk, bias_v, bias_out, turns, identity, masks, x1):
    ctx = ExitStack()
    with ctx:
        def sb(name, shape, dt=F32):
            return ctx.enter_context(nc.sbuf_tensor(name, shape, dt))

        def ps(name, shape, dt=F32):
            return ctx.enter_context(nc.psum_tensor(name, shape, dt))

        def sem(name):
            return ctx.enter_context(nc.semaphore(name))

        wqkv_sb = sb("wqkv_sb", [D, 3 * FEATS])
        wout_sb = sb("wout_sb", [128, PAIRS, D])
        bqk_sb = sb("bqk_sb", [128, 2 * QUADS * 2])
        bv_sb = sb("bv_sb", [128, PAIRS])
        bout_sb = sb("bout_sb", [1, D])
        bsum_sb = sb("bsum_sb", [1, D])
        ball_sb = sb("ball_sb", [128, TILES, D])
        turn_sb = sb("turn_sb", [128, 2, 2, COLS])
        ident = sb("ident", [128, 128])
        ident_h = sb("ident_h", [128, 128], BF16)
        mask_sb = sb("mask_sb", [128, 2, 2, 128], BF16)
        pick = sb("pick", [4, 4, 128], F32R)
        ones_f = sb("ones_f", [128, HEAD_DIM])
        ones_row = sb("ones_row", [1, 128])
        eps_col = sb("eps_col", [128, 1])
        spacer = sb("spacer", [128, 1])
        x_in = [sb(f"x_in{i}", [128, TILES, D]) for i in range(2)]
        x_res = [sb(f"x_res{i}", [128, TILES, D]) for i in range(2)]
        stat_in = sb("stat_in", [128, TILES, 6])
        mv_in = sb("mv_in", [128, TILES, 2])
        ln_in = sb("ln_in", [128, TILES])
        rstd_in = sb("rstd_in", [128, TILES])
        x_norm = sb("x_norm", [128, TILES, D])
        x_normT = [sb(f"x_normT{i}", [D, COLS]) for i in range(2)]
        stage = sb("stage", [128, 2, 2, QUADS, 2, COLS], F32R)
        stack = [sb(f"stack{i}", [128, 3, HEADS, COLS], F32R) for i in range(2)]
        v_sb = sb("v_sb", [128, TILES, FEATS])
        turned_a = [sb(f"turned_a{i}", [128, 2, COLS]) for i in range(2)]
        turned_b = [sb(f"turned_b{i}", [128, 2, COLS]) for i in range(2)]
        rotated = [sb(f"rotated{i}", [128, 2, COLS]) for i in range(2)]
        neg_max = sb("neg_max", [128, TILES, 4])
        neg_maxT = sb("neg_maxT", [4, COLS], F32R)
        probs = [sb(f"probs{i}", [128, 3 * COLS]) for i in range(2)]
        log_sum = sb("log_sum", [128, COLS])
        inv_sum = sb("inv_sum", [128, COLS])
        heads_T = sb("heads_T", [128, PAIRS, COLS])
        att = sb("att", [128, TILES, D])
        stat_out = sb("stat_out", [128, TILES, 6])
        mv_out = sb("mv_out", [128, TILES, 2])
        ln_out = sb("ln_out", [128, TILES])
        rstd_out = sb("rstd_out", [128, TILES])
        x_new = [sb(f"x_new{i}", [128, TILES, D]) for i in range(2)]

        masks_f = probs[0][:, 0:512].rearrange("p (a b c) -> p a b c", a=2, b=2)

        misc = [ps(f"misc{i}", [128, 512]) for i in range(2)]
        scores = ps("scores", [128, 1024])
        shifted = ps("shifted", [128, 1024])
        head_out = ps("head_out", [128, 512])
        head_sum = ps("head_sum", [128, 512])

        const_loaded = sem("const_loaded")
        const_made = sem("const_made")
        const_act = sem("const_act")
        bias_ready = sem("bias_ready")
        bv_product = sem("bv_product")
        bsum_made = sem("bsum_made")
        ln_stat = sem("ln_stat")
        x_loaded = [sem(f"x_loaded{i}") for i in range(2)]
        res_loaded = [sem(f"res_loaded{i}") for i in range(2)]
        x_stored = [sem(f"x_stored{i}") for i in range(2)]
        ln_step = sem("ln_step")
        ln_root = sem("ln_root")
        xT_ready = sem("xT_ready")
        xT_copied = sem("xT_copied")
        qk_ready = sem("qk_ready")
        turned = sem("turned")
        rotated_done = sem("rotated_done")
        hi_done = sem("hi_done")
        lo_q_done = sem("lo_q_done")
        lo_k_done = sem("lo_k_done")
        stacked = sem("stacked")
        v_ready = sem("v_ready")
        v_copied = sem("v_copied")
        scores_ready = sem("scores_ready")
        max_done = sem("max_done")
        maxT_ready = sem("maxT_ready")
        maxT_copied = sem("maxT_copied")
        shifted_ready = sem("shifted_ready")
        probs_ready = sem("probs_ready")
        pv_ready = sem("pv_ready")
        inv_step = sem("inv_step")
        heads_done = sem("heads_done")
        out_ready = sem("out_ready")
        out_step = sem("out_step")
        out_root = sem("out_root")

        MISC = {0: [], 1: ["out", "v2"], 2: ["v3"], 3: ["xT"], 4: ["q0", "k0"], 5: ["q1", "k1"],
                6: ["v0", "q2", "k2"], 7: ["v1", "q3", "k3"]}
        ORDER = [job for u in range(8) for job in MISC[u]]
        BANK = {job: i % 2 for i, job in enumerate(ORDER)}

        def row_of(job, b):
            return b + {"out": -1, "v2": 0, "v3": 0, "v0": 1, "v1": 1}.get(job, 2)

        def wait_bank(pe, job, b):
            i, at = ORDER.index(job), b
            while True:
                i -= 2
                if i < 0:
                    i, at = i + len(ORDER), at + -1
                before = ORDER[i]
                row = row_of(before, at)
                if row.exists():
                    break
                if at.static and at.number() < -3:
                    return
            if before == "out":
                wait(pe, out_step, row.count(5, 1))
            elif before == "xT":
                wait(pe, xT_copied, row.count(1, 1))
            elif before[0] == "v":
                wait(pe, v_copied, row.count(4, int(before[1]) + 1))
            else:
                chunk = 2 * int(before[1]) + (before[0] == "k")
                wait(pe, turned, row.count(16, 2 * chunk + 2))

        def steps(engine, run):
            for b in range(-2, 4):
                run(Row(0, b))
            with engine.Fori(2, ROWS // 2 - 1) as pair:
                run(Row(pair, 0))
                run(Row(pair, 1))
            for b in range(ROWS - 2, ROWS + 1):
                run(Row(0, b))

        def next_quad(b, g):
            return (b, g + 1) if g < 3 else (b + 1, 0)

        block = ctx.enter_context(nc.Block())

        @block.sync
        def _(sp):
            for dst, src in ((wqkv_sb[:, :], w_qkv), (wout_sb[:, :, :], w_out), (bqk_sb[:, :], bias_qk),
                             (bv_sb[:, :], bias_v), (bout_sb[:, :], bias_out), (turn_sb[:, :, :, :], turns),
                             (ident[:, :], identity), (masks_f, masks)):
                sp.dma_start(dst, src).then_inc(const_loaded, 16)

            def load_x(row):
                wait(sp, ln_step, (row + -2).count(3, 3))
                sp.dma_start(x_in[row.parity][:, :, :], x[row.number()]).then_inc(x_loaded[row.parity], 16)

            def step(b):
                nxt, prev = b + 1, b + -1
                if (b + 2).exists():
                    load_x(b + 2)
                if b.exists():
                    wait(sp, out_step, (b + -2).count(5, 5))
                    sp.dma_start(x_res[b.parity][:, :, :], x[b.number()]).then_inc(res_loaded[b.parity], 16)
                if nxt.exists():
                    stack_when = ((hi_done, nxt.count(8, 8)), (lo_q_done, nxt.count(4, 4)), (lo_k_done, nxt.count(4, 4)),
                                  (shifted_ready, (nxt + -2).count(8, 8)))
                    if not nxt.static:
                        stack_when = [(semaphore, sp.to_reg(count)) for semaphore, count in stack_when]
                    for semaphore, count in stack_when:
                        wait(sp, semaphore, count)
                    to = stack[nxt.parity]
                    for part in (HI, LO):
                        for half in range(2):
                            for h in range(4):
                                src = stage[32 * h:32 * h + 32, part, :, :, half, :].bitcast(F32)
                                p = 64 * part + 32 * half
                                sp.dma_start(to[p:p + 32, 0:2, h::4, :].bitcast(F32), src).then_inc(stacked, 16)
                                p = 64 * (1 - part) + 32 * half
                                sp.dma_start(to[p:p + 32, K_SWAPPED, h::4, :].bitcast(F32), src[:, 1]).then_inc(stacked, 16)
                if prev.exists():
                    wait(sp, out_step, prev.count(5, 5))
                    sp.dma_start(x1[prev.number()], x_new[prev.parity][:, :, :]).then_inc(x_stored[prev.parity], 16)

            steps(sp, step)
            for i in range(2):
                sp.wait_ge(x_stored[i], 16 * (ROWS // 2))

        @block.gpsimd
        def _(pool):
            def step(b):
                new = b + 2
                if not new.exists():
                    return
                for chunk in range(8):
                    quad, side = divmod(chunk, 2)
                    pool.wait_ge(turned, new.count(16, 2 * chunk + 2))
                    wait(pool, hi_done, new.count(8, chunk - 1))
                    wait(pool, (lo_q_done, lo_k_done)[side], new.count(4, quad))
                    pool.tensor_tensor(rotated[side][:, :, :], turned_a[side][:, :, :], turned_b[side][:, :, :], ALU.add).then_inc(rotated_done, 1)
                    if side == 1:
                        pool.wait_ge(hi_done, new.count(8, chunk + 1))
                        if quad == 0:
                            wait(pool, stacked, (new + -1).count(16 * STACK_DMAS, 16 * STACK_DMAS))
                        pool.wait_ge(rotated_done, new.count(8, chunk + 1))
                        pool.tensor_tensor(stage[:, LO, side, quad, :, :], rotated[side][:, :, :],
                                           stage[:, HI, side, quad, :, :].bitcast(F32), ALU.subtract).then_inc(lo_k_done, 1)

            steps(pool, step)

        @block.scalar
        def _(act):
            act.preload_act_table_set("natural_log_exp_and_others")
            act.wait_ge(bias_ready, 1)
            for t in range(TILES):
                act.activation(ball_sb[:, t, :], misc[1][:, 0:D], ACT.Copy).then_inc(const_act, 1)

            def root(mean_var, out_log, out, done, row):
                act.activation(out_log[:, :], mean_var[:, :, 1], ACT.Ln, bias=eps_col[:, 0:1]).then_inc(done, 1)
                act.wait_ge(done, row.count(2, 1))
                act.activation(out[:, :], out_log[:, :], ACT.Exp, scale=-0.5).then_inc(done, 1)

            def invert_sums(row, u):
                act.wait_ge(pv_ready, row.count(8, u + 1))
                act.activation(log_sum[:, :], head_sum[:, 0:COLS], ACT.Ln).then_inc(inv_step, 1)
                wait(act, heads_done, row.count(8, u))
                act.wait_ge(inv_step, row.count(16, 2 * u + 1))
                act.activation(inv_sum[:, :], log_sum[:, :], ACT.Exp, scale=-1.0).then_inc(inv_step, 1)

            act.wait_ge(const_made, 1)

            def step(b):
                nxt, prev, new = b + 1, b + -1, b + 2
                for u in range(8):
                    for job in MISC[u]:
                        row = row_of(job, b)
                        if job[0] == "v" and row.exists():
                            half, t = divmod(int(job[1]), 2)
                            act.wait_ge(v_ready, row.count(4, int(job[1]) + 1))
                            wait(act, pv_ready, (row + -1).count(8, 4 * half + 4))
                            act.activation(v_sb[:, t, half * 512:half * 512 + 512], misc[BANK[job]][:, :],
                                           ACT.Copy).then_inc(v_copied, 1)
                    if u == 1 and new.exists():
                        act.wait_ge(ln_step, new.count(3, 1))
                        root(mv_in, ln_in, rstd_in, ln_root, new)
                    if u == 3 and new.exists():
                        act.wait_ge(xT_ready, new.count(1, 1))
                        act.activation(x_normT[new.parity][:, :], misc[BANK["xT"]][:, 0:COLS], ACT.Copy).then_inc(xT_copied, 1)
                    if b.exists():
                        act.wait_ge(shifted_ready, b.count(8, u + 1))
                        wait(act, pv_ready, b.count(8, u - 1))
                        act.activation(probs[u % 2][:, :], shifted[:, 0:3 * COLS], ACT.Exp,
                                       scale=HEAD_DIM ** -0.5).then_inc(probs_ready, 1)
                    if u >= 4 and new.exists():
                        for side in range(2):
                            chunk = 2 * (u - 4) + side
                            act.wait_ge(rotated_done, new.count(8, chunk + 1))
                            if chunk == 0:
                                wait(act, stacked, (new + -1).count(16 * STACK_DMAS, 16 * STACK_DMAS))
                            act.activation(stage[:, HI, side, u - 4, :, :], rotated[side][:, :, :], ACT.Copy).then_inc(hi_done, 1)
                    if u > 0 and b.exists():
                        invert_sums(b, u - 1)
                    if u == 0 and prev.exists():
                        invert_sums(prev, 7)
                    if u == 1 and prev.exists():
                        act.wait_ge(out_step, prev.count(5, 3))
                        root(mv_out, ln_out, rstd_out, out_root, prev)

            steps(act, step)

        @block.vector
        def _(dve):
            dve.wait_ge(const_loaded, 16 * 8)
            dve.memset(ones_f[:, :], 1.0)
            dve.memset(ones_row[:, :], 1.0)
            dve.memset(eps_col[:, :], EPS)
            dve.tensor_copy(ident_h[:, :], ident[:, :])
            dve.tensor_copy(mask_sb[:, :, :, :], masks_f)
            for i in range(4):
                last = dve.tensor_copy(pick[:, i, :], ident[0:4, i:i + 1].to_broadcast([4, 128]))
            last.then_inc(const_made, 1)
            dve.wait_ge(bv_product, 1)
            dve.tensor_tensor(bsum_sb[:, :], misc[0][0:1, 0:D], bout_sb[:, :], ALU.add).then_inc(bsum_made, 1)

            def normalise(row):
                dve.wait_ge(x_loaded[row.parity], row.count_of_parity(16, 16))
                xs = x_in[row.parity]
                for t in range(TILES):
                    last = dve.bn_stats(stat_in[:, t, :], xs[:, t, :])
                last.then_inc(ln_stat, 1)
                wait_apart(dve, ln_stat, row.count(1, 1), spacer[:, :])
                for t in range(TILES):
                    last = dve.bn_aggr(mv_in[:, t, :], stat_in[:, t, :])
                last.then_inc(ln_step, 1)

            def normalise_end(row):
                xs = x_in[row.parity]
                dve.wait_ge(ln_root, row.count(2, 2))
                wait(dve, xT_ready, row.count(1, 0))
                for t in range(TILES):
                    last = dve.tensor_scalar(x_norm[:, t, :], xs[:, t, :], mv_in[:, t, 0:1], rstd_in[:, t:t + 1],
                                             ALU.subtract, ALU.mult)
                    last.then_inc(ln_step, 1)

            def turn(row, chunk):
                quad, side = divmod(chunk, 2)
                bank = misc[BANK["qk"[side] + str(quad)]]
                dve.wait_ge(qk_ready, row.count(8, chunk + 1))
                wait(dve, rotated_done, row.count(8, chunk - 1))
                for half, to in ((0, turned_a[side]), (1, turned_b[side])):
                    col = (side * QUADS + quad) * 2 + half
                    part = bank[:, half * COLS:(half + 1) * COLS].unsqueeze(1).to_broadcast([128, 2, COLS])
                    dve.scalar_tensor_tensor(out=to[:, :, :], in0=part, scalar=bqk_sb[:, col:col + 1],
                                             in1=turn_sb[:, half, :, :], op0=ALU.add, op1=ALU.mult).then_inc(turned, 1)

            def low_half_q(row, quad):
                dve.wait_ge(hi_done, row.count(8, 2 * quad + 1))
                if quad == 0:
                    wait(dve, stacked, (row + -1).count(16 * STACK_DMAS, 16 * STACK_DMAS))
                dve.tensor_tensor(stage[:, LO, Q_SIDE, quad, :, :], rotated[0][:, :, :],
                                  stage[:, HI, Q_SIDE, quad, :, :].bitcast(F32), ALU.subtract).then_inc(lo_q_done, 1)

            def scale_heads(row, u):
                dve.wait_ge(inv_step, row.count(16, 2 * u + 2))
                dve.wait_ge(pv_ready, row.count(8, u + 1))
                if u == 0:
                    wait(dve, out_ready, row.count(1, 0))
                dve.tensor_tensor(heads_T[:, u, :], head_out[:, 0:COLS], inv_sum[:, :], ALU.mult).then_inc(heads_done, 1)

            def finish(row):
                bank = misc[BANK["out"]]
                dve.wait_ge(out_ready, row.count(1, 1))
                dve.tensor_tensor(att[:, :, :], bank[:, 0:TILES * D].rearrange("p (t d) -> p t d", t=TILES),
                                  ball_sb[:, :, :], ALU.add).then_inc(out_step, 1)
                dve.wait_ge(out_step, row.count(5, 1))
                for t in range(TILES):
                    last = dve.bn_stats(stat_out[:, t, :], att[:, t, :])
                last.then_inc(out_step, 1)
                wait_apart(dve, out_step, row.count(5, 2), spacer[:, :])
                for t in range(TILES):
                    last = dve.bn_aggr(mv_out[:, t, :], stat_out[:, t, :])
                last.then_inc(out_step, 1)

            def finish_end(row):
                dve.wait_ge(out_root, row.count(2, 2))
                for t in range(TILES):
                    last = dve.tensor_scalar(att[:, t, :], att[:, t, :], mv_out[:, t, 0:1], rstd_out[:, t:t + 1],
                                             ALU.subtract, ALU.mult)
                last.then_inc(out_step, 1)
                dve.wait_ge(out_step, row.count(5, 4))
                dve.wait_ge(res_loaded[row.parity], row.count_of_parity(16, 16))
                wait(dve, x_stored[row.parity], row.count_of_parity(16, 0))
                dve.tensor_tensor(x_new[row.parity][:, :, :], att[:, :, :], x_res[row.parity][:, :, :],
                                  ALU.add).then_inc(out_step, 1)

            dve.wait_ge(const_act, 2)

            def step(b):
                nxt, prev, new = b + 1, b + -1, b + 2
                for u in range(8):
                    g, pair = divmod(u, 2)
                    if u == 1 and new.exists():
                        normalise(new)
                    if u == 2 and new.exists():
                        normalise_end(new)
                    if u >= 4 and new.exists():
                        turn(new, 2 * (u - 4))
                        turn(new, 2 * (u - 4) + 1)
                    if u == 1 and prev.exists():
                        finish(prev)
                    if u == 2 and prev.exists():
                        finish_end(prev)
                    row, quad = next_quad(b, g)
                    if row.exists() and (b.exists() or g == 3):
                        n = 2 * quad + pair
                        dve.wait_ge(scores_ready, row.count(8, n + 1))
                        if pair == 0:
                            wait(dve, maxT_ready, row.count(4, quad))
                        dve.tensor_reduce(neg_max[:, 1, 2 * pair:2 * pair + 2],
                                          scores[:, 0:512].rearrange("p (h k) -> p h k", h=2), AXIS_X, ALU.max, negate=True)
                        dve.tensor_reduce(neg_max[:, 0, 2 * pair:2 * pair + 2],
                                          scores[:, 512:768].rearrange("p (h k) -> p h k", h=2), AXIS_X, ALU.max,
                                          negate=True).then_inc(max_done, 1)
                    if u >= 4 and new.exists():
                        low_half_q(new, u - 4)
                    if pair == 1 and row.exists() and (b.exists() or g == 3):
                        dve.wait_ge(maxT_ready, row.count(4, quad + 1))
                        dve.tensor_copy(neg_maxT[:, :], scores[0:4, 768:1024]).then_inc(maxT_copied, 1)
                    if u > 0 and b.exists():
                        scale_heads(b, u - 1)
                    if u == 0 and prev.exists():
                        scale_heads(prev, 7)

            steps(dve, step)

        @block.tensor
        def _(pe):
            pe.wait_ge(const_loaded, 16 * 8)
            for p in range(PAIRS):
                last = pe.matmul(misc[0][0:1, 0:D], bv_sb[:, p:p + 1], wout_sb[:, p, :], start=p == 0, stop=p == PAIRS - 1)
            last.then_inc(bv_product, 1)
            pe.wait_ge(bsum_made, 1)
            pe.matmul(misc[1][:, 0:D], ones_row[:, :], bsum_sb[:, :], start=True, stop=True).then_inc(bias_ready, 1)
            pe.wait_ge(const_act, 2)

            def project(job, b):
                row = row_of(job, b)
                if not row.exists():
                    return
                bank = misc[BANK[job]]
                wait_bank(pe, job, b)
                if job == "out":
                    pe.wait_ge(heads_done, row.count(8, 8))
                    for t in range(TILES):
                        for p in range(PAIRS):
                            last = pe.matmul(bank[:, t * D:(t + 1) * D], heads_T[:, p, 128 * t:128 * t + 128],
                                             wout_sb[:, p, :], start=p == 0, stop=p == PAIRS - 1)
                    last.then_inc(out_ready, 1)
                elif job == "xT":
                    pe.wait_ge(ln_step, row.count(3, 3))
                    for t in range(TILES):
                        last = pe.transpose(bank[:, 128 * t:128 * t + 128], x_norm[:, t, :], ident[:, :])
                    last.then_inc(xT_ready, 1)
                elif job[0] == "v":
                    pe.wait_ge(xT_copied, row.count(1, 1))
                    half, t = divmod(int(job[1]), 2)
                    at = 2 * FEATS + 512 * half
                    pe.matmul(bank[:, :], x_normT[row.parity][:, 128 * t:128 * t + 128], wqkv_sb[:, at:at + 512],
                              start=True, stop=True).then_inc(v_ready, 1)
                else:
                    pe.wait_ge(xT_copied, row.count(1, 1))
                    side = int(job[0] == "k")
                    for half in range(2):
                        at = ((side * QUADS + int(job[1])) * 2 + half) * 128
                        last = pe.matmul(bank[:, half * COLS:(half + 1) * COLS], wqkv_sb[:, at:at + 128],
                                         x_normT[row.parity][:, :], start=half == 0, stop=half == 1, skip_group_check=True)
                    last.then_inc(qk_ready, 1)

            def score(row, quad, pair):
                n = 2 * quad + pair
                if n == 0:
                    pe.wait_ge(stacked, row.count(16 * STACK_DMAS, 16 * STACK_DMAS))
                wait(pe, max_done, row.count(8, n))
                if pair == 0:
                    wait(pe, maxT_copied, row.count(4, quad))
                s = stack[row.parity]
                for t, at, keys in ((1, 0, 256), (0, 512, 128)):
                    for i in range(2):
                        h = 4 * quad + 2 * pair + i
                        out = scores[:, at + i * keys:at + (i + 1) * keys]
                        for n_k, k in enumerate((K_SIDE, K_SWAPPED)):
                            pe.matmul(out, s[:, Q_SIDE, h, 128 * t:128 * t + 128], s[:, k, h, 0:keys],
                                      start=i == 0 and n_k == 0, stop=False, skip_group_check=True)
                    diagonal = scores[:, at:at + 2 * keys].rearrange("p (h k) -> p h k", h=2)[:, :, keys - 128:keys]
                    last = pe.matmul(diagonal, ident_h[:, :], mask_sb[:, 0, :, :], start=False, stop=True,
                                     skip_group_check=True)
                last.then_inc(scores_ready, 1)

            def turn_maxima(row, quad):
                pe.wait_ge(max_done, row.count(8, 2 * quad + 2))
                for t in range(TILES):
                    last = pe.transpose(scores[0:4, 768 + 128 * t:768 + 128 * t + 128], neg_max[:, t, :], ident[:, :])
                last.then_inc(maxT_ready, 1)

            def score_shifted(row, quad, pair):
                u = 2 * quad + pair
                if pair == 0:
                    pe.wait_ge(maxT_copied, row.count(4, quad + 1))
                wait(pe, probs_ready, row.count(8, u))
                s = stack[row.parity]
                for t, at, first in ((0, 0, 0), (1, 512, 128)):
                    queries = COLS - first
                    for i in range(2):
                        h = 4 * quad + 2 * pair + i
                        out = shifted[:, at + i * queries:at + (i + 1) * queries]
                        pe.matmul(out, pick[:, 2 * pair + i, :], neg_maxT[:, first:COLS], start=i == 0, stop=False,
                                  skip_group_check=True)
                        for k in (K_SIDE, K_SWAPPED):
                            pe.matmul(out, s[:, k, h, 128 * t:128 * t + 128], s[:, Q_SIDE, h, first:COLS],
                                      start=False, stop=False, skip_group_check=True)
                    diagonal = shifted[:, at:at + 2 * queries].rearrange("p (h q) -> p h q", h=2)[:, :, 0:128]
                    last = pe.matmul(diagonal, ident_h[:, :], mask_sb[:, 1, :, :], start=False, stop=True,
                                     skip_group_check=True)
                last.then_inc(shifted_ready, 1)

            def weigh_values(row, u):
                pe.wait_ge(probs_ready, row.count(8, u + 1))
                if u % 4 == 0:
                    pe.wait_ge(v_copied, row.count(4, u // 2 + 2))
                wait(pe, heads_done, row.count(8, u))
                p, v = probs[u % 2], v_sb
                for t, at, first in ((0, 0, 0), (1, 512, 128)):
                    queries = COLS - first
                    for to, is_sum in ((head_out, False), (head_sum, True)):
                        for i in range(2):
                            h = 2 * u + i
                            lhs = ones_f[:, :] if is_sum else v[:, t, h * HEAD_DIM:(h + 1) * HEAD_DIM]
                            last = pe.matmul(to[64 * i:64 * i + 64, first:COLS], lhs,
                                             p[:, at + i * queries:at + (i + 1) * queries],
                                             start=t == 0, stop=t == 1)
                last.then_inc(pv_ready, 1)

            def step(b):
                prev = b + -1
                for u in range(8):
                    g, pair = divmod(u, 2)
                    for job in MISC[u]:
                        project(job, b)
                    if b.exists():
                        score_shifted(b, g, pair)
                    row, quad = next_quad(b, g)
                    ahead = row.exists() and (b.exists() or g == 3)
                    if ahead:
                        score(row, quad, pair)
                    if u > 0 and b.exists():
                        weigh_values(b, u - 1)
                    if u == 0 and prev.exists():
                        weigh_values(prev, 7)
                    if pair == 1 and ahead:
                        turn_maxima(row, quad)

            pe.wait_ge(const_made, 1)
            steps(pe, step)


def second_part(nc, x1, out, w_in2, b_in2, w_out2, b_out2, ln_cols, router, w1, w2, identity, head_masks,
                value_mask, mask32, tri):
    ctx = ExitStack()
    with ctx:
        def sb(name, shape, dt=F32):
            return ctx.enter_context(nc.sbuf_tensor(name, shape, dt))

        def ps(name, shape, dt=F32):
            return ctx.enter_context(nc.psum_tensor(name, shape, dt))

        def sem(name):
            return ctx.enter_context(nc.semaphore(name))

        win_sb = sb("win_sb", [D, 3 * D])
        bin_sb = sb("bin_sb", [128, 3])
        wo2_sb = sb("wo2_sb", [D, D])
        bo2_sb = sb("bo2_sb", [128, D])
        ln_sb = sb("ln_sb", [128, 4])
        router_sb = sb("router_sb", [D, EXPERTS])
        w1_sb = sb("w1_sb", [D, EXPERTS, FF])
        w2_sb = sb("w2_sb", [128, EXPERTS, 2, D])
        id_sb = sb("id_sb", [128, 128])
        id_half = sb("id_half", [128, 128], BF16)
        hm_sb = sb("hm_sb", [128, 2, 4])
        bias_x = sb("bias_x", [128, 2, 4])
        vm_sb = sb("vm_sb", [128, D])
        m32_f = sb("m32_f", [128, 16, ROWS])
        m32_sb = sb("m32_sb", [128, 16, ROWS], BF16)
        tri_sb = sb("tri_sb", [128, EXPERTS, EXPERTS])
        half_neg = sb("half_neg", [128, CT])
        eps_ct = sb("eps_ct", [128, CT])
        spacer = sb("spacer_b", [128, 1])
        e_base = sb("e_base", [128, CT, EXPERTS])
        xb = [sb(f"xb{i}", [128, CT, D]) for i in range(2)]
        xr = [sb(f"xr{i}", [128, CT, D]) for i in range(2)]
        st1 = sb("st1", [128, CT, 6])
        mv1 = sb("mv1", [128, CT, 2])
        root1 = sb("root1", [128, 7, CT])
        y0 = [sb(f"y0_{i}", [128, CT, D]) for i in range(2)]
        z1 = sb("z1", [128, CT, D])
        hnT = sb("hnT", [D, TOK])
        q_x = sb("q_x", [D, CC, 4, ROWS])
        k_x = sb("k_x", [D, CC, 4, ROWS])
        v_x = sb("v_x", [128, CC, D])
        smax = sb("smax", [128, CC, 4])
        s_sub = sb("s_sub", [128, CC, 4, ROWS])
        p_exp = sb("p_exp", [128, CC, 4, ROWS])
        p_sum = sb("p_sum", [128, CC, 4])
        p_inv = sb("p_inv", [128, CC, 4])
        p_T = sb("p_T", [128, CC, 4, ROWS])
        oT = sb("oT", [D, TOK])
        acc = [sb(f"acc{i}", [128, CT, D]) for i in range(2)]
        st2 = sb("st2", [128, CT, 6])
        mv2 = sb("mv2", [128, CT, 2])
        root2 = sb("root2", [128, 2, CT])
        z2 = sb("z2", [128, CT, D])
        hn2T = sb("hn2T", [D, TOK])
        l_max = sb("l_max", [128, CT])
        l_sub = sb("l_sub", [128, CT, EXPERTS])
        r_exp = sb("r_exp", [128, CT, EXPERTS])
        r_sum = sb("r_sum", [128, CT])
        r_inv = sb("r_inv", [128, CT])
        r_prob = sb("r_prob", [128, CT, EXPERTS])
        above = sb("above", [128, CT, EXPERTS, EXPERTS])
        equal = sb("equal", [128, CT, EXPERTS, EXPERTS])
        rank = sb("rank", [128, CT, EXPERTS])
        gates = [sb(f"gates{i}", [128, CT, EXPERTS]) for i in range(2)]
        mid = [sb(f"mid{i}", [128, 2, TOK]) for i in range(2)]
        st3 = sb("st3", [128, CT, 6])
        mv3 = sb("mv3", [128, CT, 2])
        root3 = sb("root3", [128, 2, CT])
        fin = [sb(f"fin{i}", [128, CT, D]) for i in range(2)]

        up = [ps(f"up{i}", [128, 512]) for i in range(2)]
        down = ps("down", [128, 512])
        bank = [ps(f"bank{i}", [128, 512]) for i in range(5)]

        c_loaded = sem("c_loaded")
        c_made = sem("c_made")
        xb_loaded = [sem(f"xb_loaded{i}") for i in range(2)]
        xr_loaded = [sem(f"xr_loaded{i}") for i in range(2)]
        stored = [sem(f"stored{i}") for i in range(2)]
        ln1 = sem("ln1")
        ln1_root = sem("ln1_root")
        y0_biased = sem("y0_biased")
        t1_ready = sem("t1_ready")
        hn_copied = sem("hn_copied")
        q_ready = sem("q_ready")
        k_ready = sem("k_ready")
        q_spread = sem("q_spread")
        k_spread = sem("k_spread")
        v2_ready = sem("v2_ready")
        v_spread = sem("v_spread")
        s_ready = sem("s_ready")
        s_max = sem("s_max")
        s_less = sem("s_less")
        p_ready = sem("p_ready")
        p_step = sem("p_step")
        p_scaled = sem("p_scaled")
        o_ready = sem("o_ready")
        o_copied = sem("o_copied")
        r_ready = sem("r_ready")
        ln2 = sem("ln2")
        ln2_root = sem("ln2_root")
        t2_ready = sem("t2_ready")
        hn2_copied = sem("hn2_copied")
        l_ready = sem("l_ready")
        route = sem("route")
        route_exp = sem("route_exp")
        up_ready = sem("up_ready")
        mid_ready = sem("mid_ready")
        down_ready = sem("down_ready")
        gated = sem("gated")
        ln3 = sem("ln3")
        ln3_root = sem("ln3_root")

        USES = [("t2", -1, hn2_copied, 1, 1), ("t1", 0, hn_copied, 1, 1), ("logits", -1, route, 11, 2),
                ("q", 0, q_spread, 4, 4), ("k", 0, k_spread, 4, 4)]
        USES += [(f"v{j}", 0, v_spread, 4, j + 1) for j in range(4)]
        USES += [(f"s{j}", 0, s_less, 4, j + 1) for j in range(4)]
        USES += [("o", 0, o_copied, 1, 1), ("r", 0, ln2, 4, 1)]
        BANK = {use[0]: i % 5 for i, use in enumerate(USES)}

        def wait_bank(pe, name, i):
            n, at = [use[0] for use in USES].index(name), i
            while True:
                n -= 5
                if n < 0:
                    n, at = n + len(USES), at + -1
                _, offset, semaphore, per, event = USES[n]
                chunk = at + offset
                if chunk.exists():
                    return wait(pe, semaphore, chunk.count(per, event))
                if at.static and at.number() < -1:
                    return

        def steps(engine, run):
            for i in range(-1, 4):
                run(Row(0, i, CHUNKS))
            with engine.Fori(2, CHUNKS // 2 - 1) as pair:
                run(Row(pair, 0, CHUNKS))
                run(Row(pair, 1, CHUNKS))
            for i in range(CHUNKS - 2, CHUNKS + 2):
                run(Row(0, i, CHUNKS))

        x1_chunks = x1.rearrange("c s d -> (c s) d").rearrange("(i t p) d -> i p t d", p=128, t=CT)
        out_chunks = out.rearrange("s (i t c) d -> i c s t d", t=CT, c=4)

        block = ctx.enter_context(nc.Block())

        @block.sync
        def _(sp):
            for dst, src in ((win_sb[:, :], w_in2), (bin_sb[:, :], b_in2), (wo2_sb[:, :], w_out2),
                             (bo2_sb[:, :], b_out2), (ln_sb[:, :], ln_cols), (router_sb[:, :], router),
                             (w1_sb[:, :, :], w1), (w2_sb[:, :, :, :], w2), (id_sb[:, :], identity),
                             (hm_sb[:, :, :], head_masks), (vm_sb[:, :], value_mask), (m32_f[:, :, :], mask32),
                             (tri_sb[:, :, :], tri)):
                sp.dma_start(dst, src).then_inc(c_loaded, 16)

            def step(i):
                nxt, m, t = i + 1, i + -1, i + -2
                if nxt.exists():
                    wait(sp, ln1, (nxt + -2).count(3, 3))
                    sp.dma_start(xb[nxt.parity][:, :, :], x1_chunks[nxt.number()]).then_inc(xb_loaded[nxt.parity], 16)
                if m.exists():
                    wait(sp, ln3, (m + -2).count(4, 4))
                    sp.dma_start(xr[m.parity][:, :, :], x1_chunks[m.number()]).then_inc(xr_loaded[m.parity], 16)
                if t.exists():
                    sp.wait_ge(ln3, t.count(4, 4))
                    for c in range(4):
                        sp.dma_start(out_chunks[t.number(), c], fin[t.parity][32 * c:32 * c + 32, :, :]).then_inc(stored[t.parity], 16)

            steps(sp, step)
            for i in range(2):
                sp.wait_ge(stored[i], 64 * (CHUNKS // 2))

        @block.gpsimd
        def _(pool):
            pool.memset(half_neg[:, :], -0.5)
            pool.memset(eps_ct[:, :], EPS)
            pool.memset(e_base[:, :, :], float(np.e)).then_inc(c_made, 1)
            pool.wait_ge(c_made, 2)

            def root(variance, work, done, row, per):
                pool.tensor_tensor(work[:, 0, :], variance, eps_ct[:, :], ALU.add).then_inc(done, 1)
                pool.wait_ge(done, row.count(per, 1))
                pool.tensor_tensor(work[:, 1, :], work[:, 0, :], half_neg[:, :], ALU.pow).then_inc(done, 1)

            def step(i):
                nxt, m, t = i + 1, i + -1, i + -2
                if m.exists():
                    pool.wait_ge(route, m.count(11, 2))
                    pool.tensor_tensor(r_exp[:, :, :], e_base[:, :, :], l_sub[:, :, :], ALU.pow).then_inc(route_exp, 1)
                if t.exists():
                    pool.wait_ge(ln3, t.count(4, 2))
                    root(mv3[:, :, 1], root3, ln3_root, t, 2)
                if nxt.exists():
                    pool.wait_ge(ln1, nxt.count(3, 2))
                    root(mv1[:, :, 1], root1, ln1_root, nxt, 7)
                    for k, (a, b) in enumerate(((mv1[:, :, 1], root1[:, 1, :]), (root1[:, 2, :], root1[:, 1, :]))):
                        pool.wait_ge(ln1_root, nxt.count(7, k + 2))
                        pool.tensor_tensor(root1[:, k + 2, :], a, b, ALU.mult).then_inc(ln1_root, 1)
                    pool.wait_ge(ln1_root, nxt.count(7, 4))
                    pool.tensor_tensor(root1[:, 4, :], root1[:, 3, :], eps_ct[:, :], ALU.add).then_inc(ln1_root, 1)
                    pool.wait_ge(ln1_root, nxt.count(7, 5))
                    pool.tensor_tensor(root1[:, 5, :], root1[:, 4, :], half_neg[:, :], ALU.pow).then_inc(ln1_root, 1)
                    pool.wait_ge(ln1_root, nxt.count(7, 6))
                    pool.tensor_tensor(root1[:, 6, :], root1[:, 5, :], root1[:, 1, :], ALU.mult).then_inc(ln1_root, 1)
                if i.exists():
                    pool.wait_ge(p_step, i.count(3, 2))
                    pool.tensor_tensor(p_exp[:, :, :, :].rearrange("p c g t -> p (c g) t"),
                                       p_exp[:, :, :, :].rearrange("p c g t -> p (c g) t"),
                                       p_inv[:, :, :].rearrange("p c g -> p (c g)").unsqueeze(2).to_broadcast([128, CC * 4, ROWS]),
                                       ALU.mult).then_inc(p_scaled, 1)
                if nxt.exists():
                    pool.wait_ge(ln1, nxt.count(3, 3))
                    pool.tensor_tensor(y0[nxt.parity][:, :, :], y0[nxt.parity][:, :, :],
                                       bo2_sb[:, :].unsqueeze(1).to_broadcast([128, CT, D]), ALU.add).then_inc(y0_biased, 1)
                if i.exists():
                    pool.wait_ge(ln2, i.count(4, 3))
                    root(mv2[:, :, 1], root2, ln2_root, i, 2)

            steps(pool, step)

        @block.scalar
        def _(act):
            act.wait_ge(c_made, 2)

            def gelu(m, e):
                for half in range(2):
                    act.wait_ge(up_ready, m.count(16, 2 * e + half + 1))
                    if half == 0:
                        wait(act, down_ready, m.count(8, e - 1))
                    act.activation(mid[e % 2][:, half, :], up[half][:, :], ACT.Gelu).then_inc(mid_ready, 1)

            def step(i):
                m = i + -1
                for k in range(8):
                    if k == 0 and m.exists():
                        act.wait_ge(t2_ready, m.count(1, 1))
                        wait(act, up_ready, m.count(16, 0))
                        act.activation(hn2T[:, :], bank[BANK["t2"]][:, :], ACT.Identity, bias=ln_sb[:, 3:4],
                                       scale=ln_sb[:, 2:3]).then_inc(hn2_copied, 1)
                    if k == 0 and i.exists():
                        act.wait_ge(t1_ready, i.count(1, 1))
                        wait(act, v2_ready, i.count(4, 0))
                        act.activation(hnT[:, :], bank[BANK["t1"]][:, :], ACT.Identity, bias=ln_sb[:, 1:2],
                                       scale=ln_sb[:, 0:1]).then_inc(hn_copied, 1)
                    if m.exists():
                        gelu(m, k)
                    if k == 1 and i.exists():
                        wait(act, s_ready, i.count(4, 0))
                        for side, (name, ready, to, done) in enumerate((("q", q_ready, q_x, q_spread), ("k", k_ready, k_x, k_spread))):
                            act.wait_ge(ready, i.count(1, 1))
                            for n in range(4):
                                act.activation(to[:, :, n, :], bank[BANK[name]][:, :].rearrange("p (c s) -> p c s", c=CC),
                                               ACT.Identity, bias=bias_x[:, side, n:n + 1],
                                               scale=hm_sb[:, side, n:n + 1]).then_inc(done, 1)
                    if k == 3 and i.exists():
                        act.wait_ge(s_less, i.count(4, 4))
                        wait(act, p_step, i.count(3, 0))
                        act.activation(p_exp[:, :, :, :], s_sub[:, :, :, :], ACT.Exp, scale=HD2 ** -0.5).then_inc(p_ready, 1)
                    if k == 6 and i.exists():
                        act.wait_ge(o_ready, i.count(1, 1))
                        wait(act, r_ready, i.count(1, 0))
                        act.activation(oT[:, :], bank[BANK["o"]][:, :], ACT.Identity, bias=bin_sb[:, 2:3]).then_inc(o_copied, 1)

            steps(act, step)

        @block.vector
        def _(dve):
            dve.wait_ge(c_loaded, 16 * 13)
            dve.tensor_copy(id_half[:, :], id_sb[:, :])
            dve.tensor_copy(m32_sb[:, :, :], m32_f[:, :, :])
            for side in range(2):
                last = dve.tensor_scalar(bias_x[:, side, :], hm_sb[:, side, :], bin_sb[:, side:side + 1], None, ALU.mult)
            last.then_inc(c_made, 1)
            dve.wait_ge(c_made, 2)

            def tiles(a):
                return a.unsqueeze(2)

            def statistics(src, stats, mean_var, done, row, per, first):
                for t in range(CT):
                    last = dve.bn_stats(stats[:, t, :], src[:, t, :])
                last.then_inc(done, 1)
                wait_apart(dve, done, row.count(per, first), spacer[:, :])
                for t in range(CT):
                    last = dve.bn_aggr(mean_var[:, t, :], stats[:, t, :])
                last.then_inc(done, 1)

            def normalise(src, mean_var, root, to):
                for t in range(CT):
                    last = dve.tensor_scalar(to[:, t, :], src[:, t, :], mean_var[:, t, 0:1], root[:, t:t + 1],
                                             ALU.subtract, ALU.mult)
                return last

            def gate(m, e):
                dve.wait_ge(down_ready, m.count(8, e + 1))
                if e == 0:
                    dve.wait_ge(route, m.count(11, 11))
                else:
                    dve.wait_ge(gated, m.count(8, e))
                a = acc[m.parity]
                for t in range(CT):
                    last = dve.scalar_tensor_tensor(out=a[:, t, :], in0=down[:, t * D:(t + 1) * D],
                                                    scalar=gates[m.parity][:, t, e:e + 1], in1=a[:, t, :],
                                                    op0=ALU.mult, op1=ALU.add)
                last.then_inc(gated, 1)

            def router_math(m):
                steps_done = [0]

                def then(ins):
                    steps_done[0] += 1
                    ins.then_inc(route, 1)
                    dve.wait_ge(route, m.count(11, steps_done[0]))

                logits = bank[BANK["logits"]][:, 0:CT * EXPERTS].rearrange("p (t e) -> p t e", t=CT)
                dve.wait_ge(l_ready, m.count(1, 1))
                then(dve.tensor_reduce(l_max[:, :], logits, AXIS_X, ALU.max))
                then(dve.tensor_tensor(l_sub[:, :, :], logits, l_max[:, :].unsqueeze(2).to_broadcast([128, CT, EXPERTS]),
                                       ALU.subtract))
                dve.wait_ge(route_exp, m.count(1, 1))
                then(dve.tensor_reduce(r_sum[:, :], r_exp[:, :, :], AXIS_X, ALU.add))
                then(dve.reciprocal(r_inv[:, :], r_sum[:, :]))
                then(dve.tensor_tensor(r_prob[:, :, :], r_exp[:, :, :], r_inv[:, :].unsqueeze(2).to_broadcast([128, CT, EXPERTS]),
                                       ALU.mult))
                other = r_prob[:, :, :].unsqueeze(2).to_broadcast([128, CT, EXPERTS, EXPERTS])
                own = r_prob[:, :, :].unsqueeze(3).to_broadcast([128, CT, EXPERTS, EXPERTS])
                then(dve.tensor_tensor(above[:, :, :, :], other, own, ALU.is_gt))
                then(dve.tensor_tensor(equal[:, :, :, :], other, own, ALU.is_equal))
                then(dve.tensor_tensor(equal[:, :, :, :], equal[:, :, :, :],
                                       tri_sb[:, :, :].unsqueeze(1).to_broadcast([128, CT, EXPERTS, EXPERTS]), ALU.mult))
                then(dve.tensor_tensor(above[:, :, :, :], above[:, :, :, :], equal[:, :, :, :], ALU.add))
                then(dve.tensor_reduce(rank[:, :, :], above[:, :, :, :], AXIS_X, ALU.add))
                dve.scalar_tensor_tensor(out=gates[m.parity][:, :, :], in0=rank[:, :, :], scalar=float(TOP) - 0.5,
                                         in1=r_prob[:, :, :], op0=ALU.is_lt, op1=ALU.mult).then_inc(route, 1)

            def step(i):
                nxt, m, t = i + 1, i + -1, i + -2
                for k in range(8):
                    if k == 0:
                        if t.exists():
                            gate(t, 7)
                            dve.wait_ge(gated, t.count(8, 8))
                            statistics(acc[t.parity], st3, mv3, ln3, t, 4, 1)
                        if m.exists():
                            router_math(m)
                        if t.exists():
                            dve.wait_ge(ln3_root, t.count(2, 2))
                            wait(dve, stored[t.parity], t.count_of_parity(64, 0))
                            normalise(acc[t.parity], mv3, root3[:, 1, :], fin[t.parity]).then_inc(ln3, 1)
                            dve.wait_ge(ln3, t.count(4, 3))
                            dve.wait_ge(xr_loaded[t.parity], t.count_of_parity(16, 16))
                            dve.tensor_tensor(fin[t.parity][:, :, :], fin[t.parity][:, :, :], xr[t.parity][:, :, :],
                                              ALU.add).then_inc(ln3, 1)
                    if k >= 1 and m.exists():
                        gate(m, k - 1)
                    if k == 1 and i.exists():
                        wait(dve, o_ready, i.count(1, 0))
                        for j in range(4):
                            dve.wait_ge(v2_ready, i.count(4, j + 1))
                            dve.tensor_tensor(v_x[:, 4 * j:4 * j + 4, :], bank[BANK[f"v{j}"]][:, :].rearrange("p (c f) -> p c f", c=4),
                                              vm_sb[:, :].unsqueeze(1).to_broadcast([128, 4, D]), ALU.mult).then_inc(v_spread, 1)
                    if k == 2 and i.exists():
                        wait(dve, p_ready, i.count(1, 0))
                        for j in range(4):
                            s = bank[BANK[f"s{j}"]][:, :].rearrange("p (a b) -> p a b", b=ROWS)
                            to = smax[:, 4 * j:4 * j + 4, :].rearrange("p c g -> p (c g)")
                            dve.wait_ge(s_ready, i.count(4, j + 1))
                            dve.tensor_reduce(to, s, AXIS_X, ALU.max).then_inc(s_max, 1)
                            dve.wait_ge(s_max, i.count(4, j + 1))
                            dve.tensor_tensor(s_sub[:, 4 * j:4 * j + 4, :, :].rearrange("p c g t -> p (c g) t"), s,
                                              to.unsqueeze(2).to_broadcast([128, 16, ROWS]), ALU.subtract).then_inc(s_less, 1)
                    if k == 3 and nxt.exists():
                        dve.wait_ge(xb_loaded[nxt.parity], nxt.count_of_parity(16, 16))
                        statistics(xb[nxt.parity], st1, mv1, ln1, nxt, 3, 1)
                    if k == 4 and i.exists():
                        dve.wait_ge(p_ready, i.count(1, 1))
                        dve.tensor_reduce(p_sum[:, :, :].rearrange("p c g -> p (c g)"),
                                          p_exp[:, :, :, :].rearrange("p c g t -> p (c g) t"), AXIS_X, ALU.add).then_inc(p_step, 1)
                        dve.wait_ge(p_step, i.count(3, 1))
                        dve.reciprocal(p_inv[:, :, :], p_sum[:, :, :]).then_inc(p_step, 1)
                    if k == 4 and nxt.exists():
                        dve.wait_ge(ln1_root, nxt.count(7, 7))
                        wait(dve, t1_ready, nxt.count(1, 0))
                        normalise(xb[nxt.parity], mv1, root1[:, 1, :], y0[nxt.parity])
                        normalise(xb[nxt.parity], mv1, root1[:, 6, :], z1).then_inc(ln1, 1)
                    if k == 5 and i.exists():
                        dve.wait_ge(p_scaled, i.count(1, 1))
                        wait(dve, o_ready, i.count(1, 0))
                        dve.transpose(p_T[:, :, :, :].rearrange("p c g t -> p (c g t)"),
                                      p_exp[:, :, :, :].rearrange("p c g t -> p (c g t)")).then_inc(p_step, 1)
                    if k == 7 and i.exists():
                        dve.wait_ge(r_ready, i.count(1, 1))
                        dve.wait_ge(y0_biased, i.count(1, 1))
                        wait(dve, ln3, (i + -2).count(4, 3))
                        a = acc[i.parity]
                        dve.tensor_tensor(a[:, :, :], bank[BANK["r"]][:, :].rearrange("p (t d) -> p t d", t=CT),
                                          y0[i.parity][:, :, :], ALU.add).then_inc(ln2, 1)
                        dve.wait_ge(ln2, i.count(4, 1))
                        statistics(a, st2, mv2, ln2, i, 4, 2)
                        dve.wait_ge(ln2_root, i.count(2, 2))
                        wait(dve, t2_ready, i.count(1, 0))
                        normalise(a, mv2, root2[:, 1, :], z2).then_inc(ln2, 1)

            steps(dve, step)

        @block.tensor
        def _(pe):
            pe.wait_ge(c_loaded, 16 * 13)
            pe.wait_ge(c_made, 2)

            def first(m, e):
                if e == 0:
                    pe.wait_ge(hn2_copied, m.count(1, 1))
                for half in range(2):
                    wait(pe, mid_ready, m.count(16, 2 * e + half - 1))
                    pe.matmul(up[half][:, :], w1_sb[:, e, half * 128:half * 128 + 128], hn2T[:, :],
                              start=True, stop=True).then_inc(up_ready, 1)

            def second(m, e):
                pe.wait_ge(mid_ready, m.count(16, 2 * e + 2))
                wait(pe, gated, m.count(8, e))
                for t in range(CT):
                    for half in range(2):
                        last = pe.matmul(down[:, t * D:(t + 1) * D], mid[e % 2][:, half, 128 * t:128 * t + 128],
                                         w2_sb[:, e, half, :], start=half == 0, stop=half == 1)
                last.then_inc(down_ready, 1)

            def transposes(name, src, ready, done, row, i):
                ready()
                wait_bank(pe, name, i)
                for t in range(CT):
                    last = pe.transpose(bank[BANK[name]][:, t * 128:(t + 1) * 128], src[:, t, :], id_sb[:, :])
                last.then_inc(done, 1)

            def step(i):
                m, t = i + -1, i + -2
                for k in range(8):
                    if k == 0:
                        if m.exists():
                            transposes("t2", z2, lambda: pe.wait_ge(ln2, m.count(4, 4)), t2_ready, m, i)
                        if i.exists():
                            transposes("t1", z1, lambda: pe.wait_ge(ln1, i.count(3, 3)), t1_ready, i, i)
                        if t.exists():
                            second(t, 7)
                        if m.exists():
                            pe.wait_ge(hn2_copied, m.count(1, 1))
                            wait_bank(pe, "logits", i)
                            for n in range(CT):
                                last = pe.matmul(bank[BANK["logits"]][:, n * EXPERTS:(n + 1) * EXPERTS],
                                                 hn2T[:, 128 * n:128 * n + 128], router_sb[:, :], start=True, stop=True)
                            last.then_inc(l_ready, 1)
                    if m.exists():
                        first(m, k)
                    if k == 7 and i.exists():
                        pe.wait_ge(o_copied, i.count(1, 1))
                        wait_bank(pe, "r", i)
                        for n in range(CT):
                            last = pe.matmul(bank[BANK["r"]][:, n * D:(n + 1) * D], oT[:, 128 * n:128 * n + 128], wo2_sb[:, :],
                                             start=True, stop=True)
                        last.then_inc(r_ready, 1)
                    if k == 1 and i.exists():
                        pe.wait_ge(hn_copied, i.count(1, 1))
                        for side, (name, ready) in enumerate((("q", q_ready), ("k", k_ready))):
                            wait_bank(pe, name, i)
                            pe.matmul(bank[BANK[name]][:, :], win_sb[:, side * D:(side + 1) * D], hnT[:, :],
                                      start=True, stop=True).then_inc(ready, 1)
                    if k >= 1 and m.exists():
                        second(m, k - 1)
                    if k == 1 and i.exists():
                        for j in range(4):
                            wait_bank(pe, f"v{j}", i)
                            for n in range(4):
                                tokens = ROWS * (4 * j + n)
                                for g in range(4):
                                    last = pe.matmul(bank[BANK[f"v{j}"]][32 * g:32 * g + 32, n * D:(n + 1) * D],
                                                     hnT[:, tokens:tokens + ROWS], win_sb[:, 2 * D:3 * D],
                                                     start=True, stop=True)
                            last.then_inc(v2_ready, 1)
                    if k == 2 and i.exists():
                        pe.wait_ge(q_spread, i.count(4, 4))
                        pe.wait_ge(k_spread, i.count(4, 4))
                        for j in range(4):
                            wait_bank(pe, f"s{j}", i)
                            b = bank[BANK[f"s{j}"]]
                            pe.matmul(b[:, :], id_half[:, :], m32_sb[:, :, :], start=True, stop=False, skip_group_check=True)
                            for n in range(4):
                                c = 4 * j + n
                                last = pe.matmul(b[:, n * 128:(n + 1) * 128], q_x[:, c, :, :], k_x[:, c, :, :],
                                                 start=False, stop=True, skip_group_check=True)
                            last.then_inc(s_ready, 1)
                    if k == 6 and i.exists():
                        pe.wait_ge(p_step, i.count(3, 3))
                        pe.wait_ge(v_spread, i.count(4, 4))
                        wait_bank(pe, "o", i)
                        for c in range(CC):
                            for g in range(4):
                                last = pe.matmul(bank[BANK["o"]][32 * g:32 * g + 32, ROWS * c:ROWS * c + ROWS],
                                                 v_x[:, c, 32 * g:32 * g + 32], p_T[:, c, g, :], start=True, stop=True)
                        last.then_inc(o_ready, 1)

            steps(pe, step)


def build(nc, ins, out):
    x1 = nc.dram_tensor("x1", (COLS, ROWS, D), F32, kind="Internal").ap()
    attention_part(nc, ins["x"].rearrange("b (t p) d -> b p t d", p=128), ins["w_qkv"], ins["w_out"], ins["bias_qk"],
                   ins["bias_v"], ins["bias_out"], ins["turns"], ins["identity"], ins["masks"],
                   x1.rearrange("(t p) b d -> b p t d", p=128))
    names = ["w_in2", "b_in2", "w_out2", "b_out2", "ln_cols", "router", "w1", "w2", "identity", "head_masks",
             "value_mask", "mask32", "tri"]
    second_part(nc, x1, out, *[ins[n] for n in names])


def host_layouts(inputs):
    f = {k: np.asarray(v) for k, v in inputs.items()}
    w = f["L0_attn_W_in"]
    qk = w[:2 * FEATS].reshape(2, QUADS, 4, 2, HALF, D).transpose(5, 0, 1, 3, 2, 4).reshape(D, 2 * FEATS)
    b = f["L0_attn_b_in"]
    p = np.arange(HALF, dtype=np.float32) / np.float32(HALF - 1)
    thetas = np.float32(MIN_THETA) * np.float32(MAX_THETA / MIN_THETA) ** p
    angle = np.arange(COLS, dtype=np.float32)[None, :] / thetas[:, None]
    sin, cos = (np.tile(t(angle), (4, 1)).astype(np.float32) for t in (np.sin, np.cos))
    hidden = np.where(np.arange(128)[None, :] > np.arange(128)[:, None], np.float32(MASKED), np.float32(0))
    part = np.arange(128)

    def one_if(test):
        return test.astype(np.float32)

    return {
        "x": f["L0_attn_x"],
        "w_qkv": np.concatenate([qk, w[2 * FEATS:].T], axis=1),
        "w_out": f["L0_attn_W_out"].T.reshape(PAIRS, 128, D).transpose(1, 0, 2),
        "bias_qk": b[:2 * FEATS].reshape(2, QUADS, 4, 2, HALF).transpose(2, 4, 0, 1, 3).reshape(128, -1),
        "bias_v": b[2 * FEATS:].reshape(PAIRS, 128).T,
        "bias_out": f["L0_attn_b_out"][None, :],
        "turns": np.stack([np.stack([sin, cos], 1), np.stack([cos, -sin], 1)], 1),
        "identity": np.eye(128, dtype=np.float32),
        "w_in2": f["L0_ffn_in_proj_w"].T,
        "b_in2": f["L0_ffn_in_proj_b"].reshape(3, D).T,
        "w_out2": f["L0_ffn_out_proj_w"].T,
        "b_out2": np.tile(f["L0_ffn_out_proj_b"], (128, 1)),
        "ln_cols": np.stack([f["L0_ffn_" + n] for n in ("ln1_w", "ln1_b", "ln2_w", "ln2_b")], 1),
        "router": f["L0_ffn_router_w"].T,
        "w1": f["L0_ffn_w1"].transpose(1, 0, 2),
        "w2": f["L0_ffn_w2"].reshape(EXPERTS, 2, 128, D).transpose(2, 0, 1, 3),
        "head_masks": one_if(np.stack([(part % 32 // HD2)[:, None] == np.arange(4), (part // 32)[:, None] == np.arange(4)], 1)),
        "value_mask": one_if((part // 32)[:, None] == (np.arange(D) % 32 // HD2)[None, :]),
        "mask32": np.tile(np.where(np.arange(ROWS)[None, :] > (part % ROWS)[:, None], np.float32(MASKED), np.float32(0))[:, None, :], (1, 16, 1)),
        "tri": np.tile(one_if(np.arange(EXPERTS)[None, :] < np.arange(EXPERTS)[:, None]), (128, 1, 1)),
        "masks": np.stack([np.stack([hidden] * 2, 1), np.stack([hidden.T] * 2, 1)], 1),
    }


def kernel(**inputs):
    import concourse.bacc as _bacc
    from concourse.bass_utils import run_bass_kernel_spmd as _run

    nc = _bacc.Bacc("TRN2", target_bir_lowering=False, num_devices=1)
    arrays, ins = {}, {}
    for name, a in host_layouts(inputs).items():
        arrays[f"in_{name}"] = np.ascontiguousarray(a)
        ins[name] = nc.dram_tensor(f"in_{name}", a.shape, F32, kind="ExternalInput").ap()
    out = nc.dram_tensor("out", (ROWS, COLS, D), F32, kind="ExternalOutput").ap()
    build(nc, ins, out)
    return _run(nc, [arrays], core_ids=[0]).results[0]["out"]
```

```python
from contextlib import ExitStack

import numpy as np

import concourse.bass as bass
from concourse import mybir

ALU = mybir.AluOpType
ACT = mybir.ActivationFunctionType
AXIS_X = mybir.AxisListType.X
F32 = mybir.dt.float32
F32R = mybir.dt.float32r
BF16 = mybir.dt.bfloat16

ROWS, COLS, D = 32, 256, 128
HEADS, HEAD_DIM = 16, 64
HALF = HEAD_DIM // 2
QUADS, PAIRS = HEADS // 4, HEADS // 2
FEATS = HEADS * HEAD_DIM
TILES = COLS // 128
EPS = 1e-5
MASKED = -1e30
MIN_THETA, MAX_THETA = 1.0, 10000.0

HEADS2, HD2 = 16, 8
EXPERTS, TOP, FF = 8, 2, 256
CC = 16
TOK, CHUNKS = CC * ROWS, COLS // CC
CT = TOK // 128
BANKS = 4

HI, LO = 0, 1
Q_SIDE, K_SIDE, K_SWAPPED = 0, 1, 2
STACK_DMAS = 32


class Row:

    def __init__(self, pair, k, total=ROWS):
        self.pair, self.k, self.total = pair, k, total
        self.parity = k % 2
        self.static = isinstance(pair, int)

    def __add__(self, n):
        return Row(self.pair, self.k + n, self.total)

    def number(self):
        return self.pair * 2 + self.k

    def exists(self):
        return not self.static or 0 <= self.number() < self.total

    def count(self, per_row, k):
        return self.pair * (2 * per_row) + (self.k * per_row + k)

    def count_of_parity(self, per_row, k):
        return self.pair * per_row + (self.k // 2 * per_row + k)


def wait(engine, semaphore, value):
    if isinstance(value, int) and value <= 0:
        return
    engine.wait_ge(semaphore, value)


def wait_apart(dve, semaphore, value, spacer):
    wait(dve, semaphore, value)
    if not isinstance(value, int):
        dve.memset(spacer, 0.0)


def attention_part(nc, x, w_qkv, w_out, bias_qk, bias_v, bias_out, turns, identity, masks, x1):
    ctx = ExitStack()
    with ctx:
        def sb(name, shape, dt=F32):
            return ctx.enter_context(nc.sbuf_tensor(name, shape, dt))

        def ps(name, shape, dt=F32):
            return ctx.enter_context(nc.psum_tensor(name, shape, dt))

        def sem(name):
            return ctx.enter_context(nc.semaphore(name))

        wqkv_sb = sb("wqkv_sb", [D, 3 * FEATS])
        wout_sb = sb("wout_sb", [128, PAIRS, D])
        bqk_sb = sb("bqk_sb", [128, 2 * QUADS * 2])
        bv_sb = sb("bv_sb", [128, PAIRS])
        bout_sb = sb("bout_sb", [1, D])
        bsum_sb = sb("bsum_sb", [1, D])
        ball_sb = sb("ball_sb", [128, TILES, D])
        turn_sb = sb("turn_sb", [128, 2, 2, COLS])
        ident = sb("ident", [128, 128])
        ident_h = sb("ident_h", [128, 128], BF16)
        mask_sb = sb("mask_sb", [128, 2, 2, 128], BF16)
        pick = sb("pick", [4, 4, 128], F32R)
        ones_f = sb("ones_f", [128, HEAD_DIM])
        ones_row = sb("ones_row", [1, 128])
        eps_col = sb("eps_col", [128, 1])
        spacer = sb("spacer", [128, 1])
        x_in = [sb(f"x_in{i}", [128, TILES, D]) for i in range(2)]
        x_res = [sb(f"x_res{i}", [128, TILES, D]) for i in range(2)]
        stat_in = sb("stat_in", [128, TILES, 6])
        mv_in = sb("mv_in", [128, TILES, 2])
        ln_in = sb("ln_in", [128, TILES])
        rstd_in = sb("rstd_in", [128, TILES])
        x_norm = sb("x_norm", [128, TILES, D])
        x_normT = [sb(f"x_normT{i}", [D, COLS]) for i in range(2)]
        stage = sb("stage", [128, 2, 2, QUADS, 2, COLS], F32R)
        stack = [sb(f"stack{i}", [128, 3, HEADS, COLS], F32R) for i in range(2)]
        v_sb = sb("v_sb", [128, TILES, FEATS])
        turned_a = [sb(f"turned_a{i}", [128, 2, COLS]) for i in range(2)]
        turned_b = [sb(f"turned_b{i}", [128, 2, COLS]) for i in range(2)]
        rotated = [sb(f"rotated{i}", [128, 2, COLS]) for i in range(2)]
        neg_max = sb("neg_max", [128, TILES, 4])
        neg_maxT = sb("neg_maxT", [4, COLS], F32R)
        probs = [sb(f"probs{i}", [128, 3 * COLS]) for i in range(2)]
        probs_sum = [sb(f"probs_sum{i}", [128, 2, 128]) for i in range(2)]
        log_sum = sb("log_sum", [128, COLS])
        inv_sum = sb("inv_sum", [128, 2, COLS])
        heads_T = sb("heads_T", [128, PAIRS, COLS])
        att = sb("att", [128, TILES, D])
        stat_out = sb("stat_out", [128, TILES, 6])
        mv_out = sb("mv_out", [128, TILES, 2])
        ln_out = sb("ln_out", [128, TILES])
        rstd_out = sb("rstd_out", [128, TILES])
        x_new = [sb(f"x_new{i}", [128, TILES, D]) for i in range(2)]

        masks_f = probs[0][:, 0:512].rearrange("p (a b c) -> p a b c", a=2, b=2)

        misc = [ps(f"misc{i}", [128, 512]) for i in range(2)]
        scores = ps("scores", [128, 1024])
        shifted = ps("shifted", [128, 1024])
        head_out = ps("head_out", [128, 512])
        head_sum = ps("head_sum", [128, 512])
        pair_out = [head_out[:, 0:COLS], head_sum[:, COLS:2 * COLS]]

        wqkv_loaded = sem("wqkv_loaded")
        const_loaded = sem("const_loaded")
        const_made = sem("const_made")
        const_act = sem("const_act")
        bias_ready = sem("bias_ready")
        bv_product = sem("bv_product")
        bsum_made = sem("bsum_made")
        ln_stat = sem("ln_stat")
        x_loaded = [sem(f"x_loaded{i}") for i in range(2)]
        res_loaded = [sem(f"res_loaded{i}") for i in range(2)]
        x_stored = [sem(f"x_stored{i}") for i in range(2)]
        ln_step = sem("ln_step")
        ln_root = sem("ln_root")
        xT_ready = sem("xT_ready")
        xT_copied = sem("xT_copied")
        qk_ready = sem("qk_ready")
        turned = sem("turned")
        rotated_done = sem("rotated_done")
        hi_done = sem("hi_done")
        lo_q_done = sem("lo_q_done")
        lo_k_done = sem("lo_k_done")
        stacked = sem("stacked")
        v_ready = sem("v_ready")
        v_copied = sem("v_copied")
        scores_ready = sem("scores_ready")
        max_done = sem("max_done")
        maxT_ready = sem("maxT_ready")
        maxT_copied = sem("maxT_copied")
        shifted_ready = sem("shifted_ready")
        probs_ready = sem("probs_ready")
        keys_added = sem("keys_added")
        pv_ready = sem("pv_ready")
        sums_ready = sem("sums_ready")
        inv_step = sem("inv_step")
        heads_done = sem("heads_done")
        out_ready = sem("out_ready")
        out_step = sem("out_step")
        out_root = sem("out_root")

        MISC = {0: ["v1"], 1: ["v2"], 2: ["out", "v3"], 3: ["xT"], 4: ["q0", "k0"], 5: ["q1", "k1"],
                6: ["v0", "q2", "k2"], 7: ["q3", "k3"]}
        ORDER = [job for u in range(8) for job in MISC[u]]
        BANK = {job: i % 2 for i, job in enumerate(ORDER)}

        def row_of(job, b):
            return b + {"out": -1, "v2": 0, "v3": 0, "v0": 1, "v1": 0}.get(job, 2)

        def wait_bank(pe, job, b):
            i, at = ORDER.index(job), b
            while True:
                i -= 2
                if i < 0:
                    i, at = i + len(ORDER), at + -1
                before = ORDER[i]
                row = row_of(before, at)
                if row.exists():
                    break
                if at.static and at.number() < -3:
                    return
            if before == "out":
                wait(pe, out_step, row.count(5, 1))
            elif before == "xT":
                wait(pe, xT_copied, row.count(1, 1))
            elif before[0] == "v":
                wait(pe, v_copied, row.count(4, int(before[1]) + 1))
            else:
                chunk = 2 * int(before[1]) + (before[0] == "k")
                wait(pe, turned, row.count(16, 2 * chunk + 2))

        def steps(engine, run):
            for b in range(-2, 4):
                run(Row(0, b))
            with engine.Fori(2, ROWS // 2 - 1) as pair:
                run(Row(pair, 0))
                run(Row(pair, 1))
            for b in range(ROWS - 2, ROWS + 1):
                run(Row(0, b))

        def next_quad(b, g):
            return (b, g + 1) if g < 3 else (b + 1, 0)

        block = ctx.enter_context(nc.Block())

        @block.sync
        def _(sp):
            sp.dma_start(wqkv_sb[:, :], w_qkv).then_inc(wqkv_loaded, 16)

            def load_x(row):
                wait(sp, ln_step, (row + -2).count(3, 3))
                sp.dma_start(x_in[row.parity][:, :, :], x[row.number()]).then_inc(x_loaded[row.parity], 16)

            def step(b):
                nxt, prev = b + 1, b + -1
                if (b + 2).exists():
                    load_x(b + 2)
                if b.exists():
                    wait(sp, out_step, (b + -2).count(5, 5))
                    sp.dma_start(x_res[b.parity][:, :, :], x[b.number()]).then_inc(res_loaded[b.parity], 16)
                if nxt.exists():
                    stack_when = ((hi_done, nxt.count(8, 8)), (lo_q_done, nxt.count(4, 4)), (lo_k_done, nxt.count(4, 4)),
                                  (shifted_ready, (nxt + -2).count(8, 8)))
                    if not nxt.static:
                        stack_when = [(semaphore, sp.to_reg(count)) for semaphore, count in stack_when]
                    for semaphore, count in stack_when:
                        wait(sp, semaphore, count)
                    to = stack[nxt.parity]
                    for part in (HI, LO):
                        for half in range(2):
                            for h in range(4):
                                src = stage[32 * h:32 * h + 32, part, :, :, half, :].bitcast(F32)
                                p = 64 * part + 32 * half
                                sp.dma_start(to[p:p + 32, 0:2, h::4, :].bitcast(F32), src).then_inc(stacked, 16)
                                p = 64 * (1 - part) + 32 * half
                                sp.dma_start(to[p:p + 32, K_SWAPPED, h::4, :].bitcast(F32), src[:, 1]).then_inc(stacked, 16)
                if prev.exists():
                    wait(sp, out_step, prev.count(5, 5))
                    sp.dma_start(x1[prev.number()], x_new[prev.parity][:, :, :]).then_inc(x_stored[prev.parity], 16)

            steps(sp, step)
            for i in range(2):
                sp.wait_ge(x_stored[i], 16 * (ROWS // 2))

        @block.gpsimd
        def _(pool):
            def turn_sum(new, chunk):
                quad, side = divmod(chunk, 2)
                pool.wait_ge(turned, new.count(16, 2 * chunk + 2))
                wait(pool, hi_done, new.count(8, chunk - 1))
                wait(pool, (lo_q_done, lo_k_done)[side], new.count(4, quad))
                pool.tensor_tensor(rotated[side][:, :, :], turned_a[side][:, :, :], turned_b[side][:, :, :], ALU.add).then_inc(rotated_done, 1)

            def low_half_k(new, quad):
                pool.wait_ge(hi_done, new.count(8, 2 * quad + 2))
                if quad == 0:
                    wait(pool, stacked, (new + -1).count(16 * STACK_DMAS, 16 * STACK_DMAS))
                pool.wait_ge(rotated_done, new.count(8, 2 * quad + 2))
                pool.tensor_tensor(stage[:, LO, K_SIDE, quad, :, :], rotated[K_SIDE][:, :, :],
                                   stage[:, HI, K_SIDE, quad, :, :].bitcast(F32), ALU.subtract).then_inc(lo_k_done, 1)

            def add_keys(b, u):
                pool.wait_ge(probs_ready, b.count(8, u + 1))
                p = probs[u % 2]
                pool.tensor_tensor(probs_sum[u % 2][:, :, :], p[:, 0:512].rearrange("p (h q) -> p h q", h=2)[:, :, 128:256],
                                   p[:, 512:768].rearrange("p (h q) -> p h q", h=2), ALU.add).then_inc(keys_added, 1)

            def step(b):
                new = b + 2
                for u in range(8):
                    if u >= 4 and new.exists():
                        for side in range(2):
                            turn_sum(new, 2 * (u - 4) + side)
                    if b.exists():
                        add_keys(b, u)
                    if u >= 4 and new.exists():
                        low_half_k(new, u - 4)

            steps(pool, step)

        @block.scalar
        def _(act):
            for dst, src in ((ident[:, :], identity), (bqk_sb[:, :], bias_qk), (masks_f, masks), (bv_sb[:, :], bias_v),
                             (bout_sb[:, :], bias_out), (wout_sb[:, :, :], w_out), (turn_sb[:, :, :, :], turns)):
                act.dma_start(dst, src).then_inc(const_loaded, 16)
            act.preload_act_table_set("natural_log_exp_and_others")
            act.wait_ge(bias_ready, 1)
            for t in range(TILES):
                act.activation(ball_sb[:, t, :], misc[1][:, 0:D], ACT.Copy).then_inc(const_act, 1)

            def root(mean_var, out_log, out, done, row):
                act.activation(out_log[:, :], mean_var[:, :, 1], ACT.Ln, bias=eps_col[:, 0:1]).then_inc(done, 1)
                act.wait_ge(done, row.count(2, 1))
                act.activation(out[:, :], out_log[:, :], ACT.Exp, scale=-0.5).then_inc(done, 1)

            def log_sums(row, quad):
                act.wait_ge(sums_ready, row.count(4, quad + 1))
                act.activation(log_sum[:, :], head_sum[:, 0:COLS], ACT.Ln).then_inc(inv_step, 1)

            def invert_sums(row, quad, pair):
                wait(act, heads_done, row.count(8, 2 * quad + pair - 1))
                act.wait_ge(inv_step, row.count(36, 9 * quad + 1))
                for part in range(4):
                    head = 2 * pair + part // 2
                    act.activation(inv_sum[32 * part:32 * part + 32, pair, :], log_sum[32 * head:32 * head + 32, :], ACT.Exp,
                                   scale=-1.0).then_inc(inv_step, 1)

            act.wait_ge(const_made, 1)

            def step(b):
                nxt, prev, new = b + 1, b + -1, b + 2
                for u in range(8):
                    for job in MISC[u]:
                        row = row_of(job, b)
                        if job[0] == "v" and row.exists():
                            half, t = divmod(int(job[1]), 2)
                            act.wait_ge(v_ready, row.count(4, int(job[1]) + 1))
                            wait(act, pv_ready, (row + -1).count(8, 4 * half + 4))
                            act.activation(v_sb[:, t, half * 512:half * 512 + 512], misc[BANK[job]][:, :],
                                           ACT.Copy).then_inc(v_copied, 1)
                    if u == 1 and new.exists():
                        act.wait_ge(ln_step, new.count(3, 1))
                        root(mv_in, ln_in, rstd_in, ln_root, new)
                    if u == 3 and new.exists():
                        act.wait_ge(xT_ready, new.count(1, 1))
                        act.activation(x_normT[new.parity][:, :], misc[BANK["xT"]][:, 0:COLS], ACT.Copy).then_inc(xT_copied, 1)
                    done, quad = (b, u // 2 - 1) if u > 0 else (prev, 3)
                    if u % 2 == 0 and done.exists():
                        log_sums(done, quad)
                        invert_sums(done, quad, 0)
                    if b.exists():
                        act.wait_ge(shifted_ready, b.count(8, u + 1))
                        wait(act, pv_ready, b.count(8, u - 1))
                        act.activation(probs[u % 2][:, :], shifted[:, 0:3 * COLS], ACT.Exp,
                                       scale=HEAD_DIM ** -0.5).then_inc(probs_ready, 1)
                    if u >= 4 and new.exists():
                        for side in range(2):
                            chunk = 2 * (u - 4) + side
                            act.wait_ge(rotated_done, new.count(8, chunk + 1))
                            if chunk == 0:
                                wait(act, stacked, (new + -1).count(16 * STACK_DMAS, 16 * STACK_DMAS))
                            act.activation(stage[:, HI, side, u - 4, :, :], rotated[side][:, :, :], ACT.Copy).then_inc(hi_done, 1)
                    if u % 2 == 0 and done.exists():
                        invert_sums(done, quad, 1)
                    if u == 2 and prev.exists():
                        act.wait_ge(out_step, prev.count(5, 3))
                        root(mv_out, ln_out, rstd_out, out_root, prev)

            steps(act, step)

        @block.vector
        def _(dve):
            dve.wait_ge(const_loaded, 16 * 7)
            dve.memset(ones_f[:, :], 1.0)
            dve.memset(ones_row[:, :], 1.0)
            dve.memset(eps_col[:, :], EPS)
            dve.tensor_copy(ident_h[:, :], ident[:, :])
            dve.tensor_copy(mask_sb[:, :, :, :], masks_f)
            for i in range(4):
                last = dve.tensor_copy(pick[:, i, :], ident[0:4, i:i + 1].to_broadcast([4, 128]))
            last.then_inc(const_made, 1)
            dve.wait_ge(bv_product, 1)
            dve.tensor_tensor(bsum_sb[:, :], misc[0][0:1, 0:D], bout_sb[:, :], ALU.add).then_inc(bsum_made, 1)

            def normalise(row):
                dve.wait_ge(x_loaded[row.parity], row.count_of_parity(16, 16))
                xs = x_in[row.parity]
                for t in range(TILES):
                    last = dve.bn_stats(stat_in[:, t, :], xs[:, t, :])
                last.then_inc(ln_stat, 1)
                wait_apart(dve, ln_stat, row.count(1, 1), spacer[:, :])
                for t in range(TILES):
                    last = dve.bn_aggr(mv_in[:, t, :], stat_in[:, t, :])
                last.then_inc(ln_step, 1)

            def normalise_end(row):
                xs = x_in[row.parity]
                dve.wait_ge(ln_root, row.count(2, 2))
                wait(dve, xT_ready, row.count(1, 0))
                for t in range(TILES):
                    last = dve.tensor_scalar(x_norm[:, t, :], xs[:, t, :], mv_in[:, t, 0:1], rstd_in[:, t:t + 1],
                                             ALU.subtract, ALU.mult)
                    last.then_inc(ln_step, 1)

            def turn(row, chunk):
                quad, side = divmod(chunk, 2)
                bank = misc[BANK["qk"[side] + str(quad)]]
                dve.wait_ge(qk_ready, row.count(8, chunk + 1))
                wait(dve, rotated_done, row.count(8, chunk - 1))
                for half, to in ((0, turned_a[side]), (1, turned_b[side])):
                    col = (side * QUADS + quad) * 2 + half
                    part = bank[:, half * COLS:(half + 1) * COLS].unsqueeze(1).to_broadcast([128, 2, COLS])
                    dve.scalar_tensor_tensor(out=to[:, :, :], in0=part, scalar=bqk_sb[:, col:col + 1],
                                             in1=turn_sb[:, half, :, :], op0=ALU.add, op1=ALU.mult).then_inc(turned, 1)

            def low_half_q(row, quad):
                dve.wait_ge(hi_done, row.count(8, 2 * quad + 1))
                if quad == 0:
                    wait(dve, stacked, (row + -1).count(16 * STACK_DMAS, 16 * STACK_DMAS))
                dve.tensor_tensor(stage[:, LO, Q_SIDE, quad, :, :], rotated[0][:, :, :],
                                  stage[:, HI, Q_SIDE, quad, :, :].bitcast(F32), ALU.subtract).then_inc(lo_q_done, 1)

            def scale_heads(row, quad, pair):
                u = 2 * quad + pair
                dve.wait_ge(inv_step, row.count(36, 9 * quad + 4 * pair + 5))
                dve.wait_ge(pv_ready, row.count(8, u + 1))
                if u == 0:
                    wait(dve, out_ready, row.count(1, 0))
                dve.tensor_tensor(heads_T[:, u, :], pair_out[pair], inv_sum[:, pair, :], ALU.mult).then_inc(heads_done, 1)

            def finish(row):
                bank = misc[BANK["out"]]
                dve.wait_ge(out_ready, row.count(1, 1))
                dve.tensor_tensor(att[:, :, :], bank[:, 0:TILES * D].rearrange("p (t d) -> p t d", t=TILES),
                                  ball_sb[:, :, :], ALU.add).then_inc(out_step, 1)
                dve.wait_ge(out_step, row.count(5, 1))
                for t in range(TILES):
                    last = dve.bn_stats(stat_out[:, t, :], att[:, t, :])
                last.then_inc(out_step, 1)
                wait_apart(dve, out_step, row.count(5, 2), spacer[:, :])
                for t in range(TILES):
                    last = dve.bn_aggr(mv_out[:, t, :], stat_out[:, t, :])
                last.then_inc(out_step, 1)

            def finish_end(row):
                dve.wait_ge(out_root, row.count(2, 2))
                for t in range(TILES):
                    last = dve.tensor_scalar(att[:, t, :], att[:, t, :], mv_out[:, t, 0:1], rstd_out[:, t:t + 1],
                                             ALU.subtract, ALU.mult)
                last.then_inc(out_step, 1)
                dve.wait_ge(out_step, row.count(5, 4))
                dve.wait_ge(res_loaded[row.parity], row.count_of_parity(16, 16))
                wait(dve, x_stored[row.parity], row.count_of_parity(16, 0))
                dve.tensor_tensor(x_new[row.parity][:, :, :], att[:, :, :], x_res[row.parity][:, :, :],
                                  ALU.add).then_inc(out_step, 1)

            dve.wait_ge(const_act, 2)

            def copy_maxima(row, quad):
                dve.wait_ge(maxT_ready, row.count(4, quad + 1))
                dve.tensor_copy(neg_maxT[:, :], scores[0:4, 768:1024]).then_inc(maxT_copied, 1)

            def step(b):
                nxt, prev, new = b + 1, b + -1, b + 2
                for u in range(8):
                    g, pair = divmod(u, 2)
                    if pair == 0 and b.exists():
                        copy_maxima(b, g)
                    if u == 1 and new.exists():
                        normalise(new)
                    if u == 2 and new.exists():
                        normalise_end(new)
                    if u >= 4 and new.exists():
                        turn(new, 2 * (u - 4))
                    if u >= 4 and new.exists():
                        turn(new, 2 * (u - 4) + 1)
                    if u == 2 and prev.exists():
                        finish(prev)
                    if u == 3 and prev.exists():
                        finish_end(prev)
                    done, done_quad = (b, g - 1) if g > 0 else (prev, 3)
                    if pair == 0 and done.exists():
                        scale_heads(done, done_quad, 0)
                    row, quad = next_quad(b, g)
                    if row.exists() and (b.exists() or g == 3):
                        n = 2 * quad + pair
                        dve.wait_ge(scores_ready, row.count(8, n + 1))
                        if pair == 0:
                            wait(dve, maxT_ready, row.count(4, quad))
                        dve.tensor_reduce(neg_max[:, 1, 2 * pair:2 * pair + 2],
                                          scores[:, 0:512].rearrange("p (h k) -> p h k", h=2), AXIS_X, ALU.max, negate=True)
                        dve.tensor_reduce(neg_max[:, 0, 2 * pair:2 * pair + 2],
                                          scores[:, 512:768].rearrange("p (h k) -> p h k", h=2), AXIS_X, ALU.max,
                                          negate=True).then_inc(max_done, 1)
                    if u >= 4 and new.exists():
                        low_half_q(new, u - 4)
                    if pair == 0 and done.exists():
                        scale_heads(done, done_quad, 1)

            steps(dve, step)

        @block.tensor
        def _(pe):
            pe.wait_ge(const_loaded, 16 * 7)
            for p in range(PAIRS):
                last = pe.matmul(misc[0][0:1, 0:D], bv_sb[:, p:p + 1], wout_sb[:, p, :], start=p == 0, stop=p == PAIRS - 1)
            last.then_inc(bv_product, 1)
            pe.wait_ge(bsum_made, 1)
            pe.matmul(misc[1][:, 0:D], ones_row[:, :], bsum_sb[:, :], start=True, stop=True).then_inc(bias_ready, 1)
            pe.wait_ge(const_act, 2)
            pe.wait_ge(wqkv_loaded, 16)

            def project(job, b):
                row = row_of(job, b)
                if not row.exists():
                    return
                bank = misc[BANK[job]]
                wait_bank(pe, job, b)
                if job == "out":
                    pe.wait_ge(heads_done, row.count(8, 8))
                    for t in range(TILES):
                        for p in range(PAIRS):
                            last = pe.matmul(bank[:, t * D:(t + 1) * D], heads_T[:, p, 128 * t:128 * t + 128],
                                             wout_sb[:, p, :], start=p == 0, stop=p == PAIRS - 1)
                    last.then_inc(out_ready, 1)
                elif job == "xT":
                    pe.wait_ge(ln_step, row.count(3, 3))
                    for t in range(TILES):
                        last = pe.transpose(bank[:, 128 * t:128 * t + 128], x_norm[:, t, :], ident[:, :])
                    last.then_inc(xT_ready, 1)
                elif job[0] == "v":
                    pe.wait_ge(xT_copied, row.count(1, 1))
                    half, t = divmod(int(job[1]), 2)
                    at = 2 * FEATS + 512 * half
                    pe.matmul(bank[:, :], x_normT[row.parity][:, 128 * t:128 * t + 128], wqkv_sb[:, at:at + 512],
                              start=True, stop=True).then_inc(v_ready, 1)
                else:
                    pe.wait_ge(xT_copied, row.count(1, 1))
                    side = int(job[0] == "k")
                    for half in range(2):
                        at = ((side * QUADS + int(job[1])) * 2 + half) * 128
                        last = pe.matmul(bank[:, half * COLS:(half + 1) * COLS], wqkv_sb[:, at:at + 128],
                                         x_normT[row.parity][:, :], start=half == 0, stop=half == 1, skip_group_check=True)
                    last.then_inc(qk_ready, 1)

            def score(row, quad, pair):
                n = 2 * quad + pair
                if n == 0:
                    pe.wait_ge(stacked, row.count(16 * STACK_DMAS, 16 * STACK_DMAS))
                wait(pe, max_done, row.count(8, n))
                if pair == 0:
                    wait(pe, maxT_copied, row.count(4, quad))
                s = stack[row.parity]
                for t, at, keys in ((1, 0, 256), (0, 512, 128)):
                    for i in range(2):
                        h = 4 * quad + 2 * pair + i
                        out = scores[:, at + i * keys:at + (i + 1) * keys]
                        for n_k, k in enumerate((K_SIDE, K_SWAPPED)):
                            pe.matmul(out, s[:, Q_SIDE, h, 128 * t:128 * t + 128], s[:, k, h, 0:keys],
                                      start=i == 0 and n_k == 0, stop=False, skip_group_check=True)
                    diagonal = scores[:, at:at + 2 * keys].rearrange("p (h k) -> p h k", h=2)[:, :, keys - 128:keys]
                    last = pe.matmul(diagonal, ident_h[:, :], mask_sb[:, 0, :, :], start=False, stop=True,
                                     skip_group_check=True)
                last.then_inc(scores_ready, 1)

            def turn_maxima(row, quad):
                pe.wait_ge(max_done, row.count(8, 2 * quad + 2))
                for t in range(TILES):
                    last = pe.transpose(scores[0:4, 768 + 128 * t:768 + 128 * t + 128], neg_max[:, t, :], ident[:, :])
                last.then_inc(maxT_ready, 1)

            def score_shifted(row, quad, pair):
                u = 2 * quad + pair
                if pair == 0:
                    pe.wait_ge(maxT_copied, row.count(4, quad + 1))
                wait(pe, probs_ready, row.count(8, u))
                s = stack[row.parity]
                for t, at, first in ((0, 0, 0), (1, 512, 128)):
                    queries = COLS - first
                    for i in range(2):
                        h = 4 * quad + 2 * pair + i
                        out = shifted[:, at + i * queries:at + (i + 1) * queries]
                        pe.matmul(out, pick[:, 2 * pair + i, :], neg_maxT[:, first:COLS], start=i == 0, stop=False,
                                  skip_group_check=True)
                        for k in (K_SIDE, K_SWAPPED):
                            pe.matmul(out, s[:, k, h, 128 * t:128 * t + 128], s[:, Q_SIDE, h, first:COLS],
                                      start=False, stop=False, skip_group_check=True)
                    diagonal = shifted[:, at:at + 2 * queries].rearrange("p (h q) -> p h q", h=2)[:, :, 0:128]
                    last = pe.matmul(diagonal, ident_h[:, :], mask_sb[:, 1, :, :], start=False, stop=True,
                                     skip_group_check=True)
                last.then_inc(shifted_ready, 1)

            def sum_probs(row, quad):
                pe.wait_ge(probs_ready, row.count(8, 2 * quad + 2))
                wait(pe, inv_step, row.count(36, 9 * quad + -8))
                wait(pe, heads_done, row.count(8, 2 * quad))
                for t in range(TILES):
                    if t == 1:
                        pe.wait_ge(keys_added, row.count(8, 2 * quad + 2))
                    for head in range(4):
                        pair, i = divmod(head, 2)
                        of = probs[pair][:, i * COLS:i * COLS + 128] if t == 0 else probs_sum[pair][:, i, :]
                        last = pe.matmul(head_sum[32 * head:32 * head + 32, 128 * t:128 * t + 128], ones_f[:, 0:32], of,
                                         start=True, stop=True)
                last.then_inc(sums_ready, 1)

            def weigh_values(row, u):
                pe.wait_ge(probs_ready, row.count(8, u + 1))
                if u % 4 == 0:
                    pe.wait_ge(v_copied, row.count(4, u // 2 + 2))
                if u % 2 == 0:
                    wait(pe, heads_done, row.count(8, u - 1))
                else:
                    pe.wait_ge(inv_step, row.count(36, 9 * (u // 2) + 1))
                p, v = probs[u % 2], v_sb
                for t, at, first in ((0, 0, 0), (1, 512, 128)):
                    queries = COLS - first
                    for i in range(2):
                        h = 2 * u + i
                        last = pe.matmul(pair_out[u % 2][64 * i:64 * i + 64, first:COLS], v[:, t, h * HEAD_DIM:(h + 1) * HEAD_DIM],
                                  p[:, at + i * queries:at + (i + 1) * queries], start=t == 0, stop=t == 1)
                last.then_inc(pv_ready, 1)

            def step(b):
                prev = b + -1
                for u in range(8):
                    g, pair = divmod(u, 2)
                    for n, job in enumerate(MISC[u]):
                        project(job, b)
                        if n == 0 and pair == 0 and b.exists():
                            turn_maxima(b, g)
                    done, quad = (b, g - 1) if g > 0 else (prev, 3)
                    if pair == 0 and done.exists():
                        sum_probs(done, quad)
                    if b.exists():
                        score_shifted(b, g, pair)
                    row, quad = next_quad(b, g)
                    ahead = row.exists() and (b.exists() or g == 3)
                    if ahead:
                        score(row, quad, pair)
                    if u > 0 and b.exists():
                        weigh_values(b, u - 1)
                    if u == 0 and prev.exists():
                        weigh_values(prev, 7)

            pe.wait_ge(const_made, 1)
            steps(pe, step)


def second_part(nc, x1, out, w_in2, b_in2, w_out2, b_out2, ln_cols, router, w1, w2, identity, head_masks,
                value_mask, mask32, tri):
    ctx = ExitStack()
    with ctx:
        def sb(name, shape, dt=F32):
            return ctx.enter_context(nc.sbuf_tensor(name, shape, dt))

        def ps(name, shape, dt=F32):
            return ctx.enter_context(nc.psum_tensor(name, shape, dt))

        def sem(name):
            return ctx.enter_context(nc.semaphore(name))

        win_sb = sb("win_sb", [D, 3 * D])
        bin_sb = sb("bin_sb", [128, 3])
        wo2_sb = sb("wo2_sb", [D, D])
        bo2_sb = sb("bo2_sb", [128, D])
        ln_sb = sb("ln_sb", [128, 4])
        router_sb = sb("router_sb", [D, EXPERTS])
        w1_sb = sb("w1_sb", [D, EXPERTS, FF])
        w1_hl = sb("w1_hl", [D, 2, EXPERTS, FF], F32R)
        w2_sb = sb("w2_sb", [128, EXPERTS, 2, D])
        id_sb = sb("id_sb", [128, 128])
        id_half = sb("id_half", [128, 128], BF16)
        hm_sb = sb("hm_sb", [128, 2, 4])
        bias_x = sb("bias_x", [128, 2, 4])
        vm_sb = sb("vm_sb", [128, D])
        m32_f = sb("m32_f", [128, 16, ROWS])
        m32_sb = sb("m32_sb", [128, 16, ROWS], BF16)
        tri_sb = sb("tri_sb", [128, EXPERTS, EXPERTS])
        half_neg = sb("half_neg", [128, CT])
        eps_ct = sb("eps_ct", [128, CT])
        spacer = sb("spacer_b", [128, 1])
        e_base = sb("e_base", [128, CT, EXPERTS])
        xb = [sb(f"xb{i}", [128, CT, D]) for i in range(2)]
        xr = [sb(f"xr{i}", [128, CT, D]) for i in range(2)]
        st1 = sb("st1", [128, CT, 6])
        mv1 = sb("mv1", [128, CT, 2])
        root1 = sb("root1", [128, 7, CT])
        y0 = [sb(f"y0_{i}", [128, CT, D]) for i in range(2)]
        z1 = sb("z1", [128, CT, D])
        hnT = sb("hnT", [D, TOK])
        q_x = sb("q_x", [D, CC, 4, ROWS])
        k_x = sb("k_x", [D, CC, 4, ROWS])
        v_x = sb("v_x", [128, CC, D])
        smax = sb("smax", [128, CC, 4])
        s_sub = sb("s_sub", [128, CC, 4, ROWS])
        p_exp = sb("p_exp", [128, CC, 4, ROWS])
        p_sum = sb("p_sum", [128, CC, 4])
        p_inv = sb("p_inv", [128, CC, 4])
        p_T = sb("p_T", [128, CC, 4, ROWS])
        oT = sb("oT", [D, TOK])
        acc = [sb(f"acc{i}", [128, CT, D]) for i in range(2)]
        st2 = sb("st2", [128, CT, 6])
        mv2 = sb("mv2", [128, CT, 2])
        root2 = sb("root2", [128, 2, CT])
        z2 = sb("z2", [128, CT, D])
        hn2T = sb("hn2T", [D, TOK])
        hn2_hl = sb("hn2_hl", [D, 2, TOK], F32R)
        l_max = sb("l_max", [128, CT])
        l_sub = sb("l_sub", [128, CT, EXPERTS])
        r_exp = sb("r_exp", [128, CT, EXPERTS])
        r_sum = sb("r_sum", [128, CT])
        r_inv = sb("r_inv", [128, CT])
        r_prob = sb("r_prob", [128, CT, EXPERTS])
        above = sb("above", [128, CT, EXPERTS, EXPERTS])
        equal = sb("equal", [128, CT, EXPERTS, EXPERTS])
        rank = sb("rank", [128, CT, EXPERTS])
        gates = [sb(f"gates{i}", [128, CT, EXPERTS]) for i in range(2)]
        mid = [sb(f"mid{i}", [128, 2, TOK]) for i in range(2)]
        st3 = sb("st3", [128, CT, 6])
        mv3 = sb("mv3", [128, CT, 2])
        root3 = sb("root3", [128, 2, CT])
        fin = [sb(f"fin{i}", [128, CT, D]) for i in range(2)]

        up = [ps(f"up{i}", [128, 512]) for i in range(2)]
        down = [ps(f"down{i}", [128, 512]) for i in range(2)]
        bank = [ps(f"bank{i}", [128, 512]) for i in range(BANKS)]

        c_loaded = sem("c_loaded")
        w_loaded = sem("w_loaded")
        c_made = sem("c_made")
        xb_loaded = [sem(f"xb_loaded{i}") for i in range(2)]
        xr_loaded = [sem(f"xr_loaded{i}") for i in range(2)]
        stored = [sem(f"stored{i}") for i in range(2)]
        ln1 = sem("ln1")
        ln1_root = sem("ln1_root")
        y0_biased = sem("y0_biased")
        t1_ready = sem("t1_ready")
        hn_copied = sem("hn_copied")
        q_ready = sem("q_ready")
        k_ready = sem("k_ready")
        q_spread = sem("q_spread")
        k_spread = sem("k_spread")
        v2_ready = sem("v2_ready")
        v_spread = sem("v_spread")
        s_ready = sem("s_ready")
        s_max = sem("s_max")
        s_less = sem("s_less")
        p_ready = sem("p_ready")
        p_step = sem("p_step")
        o_ready = sem("o_ready")
        o_copied = sem("o_copied")
        r_ready = sem("r_ready")
        ln2 = sem("ln2")
        ln2_root = sem("ln2_root")
        t2_ready = sem("t2_ready")
        w1_split = sem("w1_split")
        hn2_hi = sem("hn2_hi")
        hn2_copied = sem("hn2_copied")
        hn2_lo = sem("hn2_lo")
        l_ready = sem("l_ready")
        route = sem("route")
        route_exp = sem("route_exp")
        up_ready = sem("up_ready")
        mid_ready = sem("mid_ready")
        down_ready = sem("down_ready")
        gated = sem("gated")
        ln3 = sem("ln3")
        ln3_root = sem("ln3_root")

        USES = [(f"s{j}", 0, s_less, 4, j + 1) for j in range(4)]
        USES += [("t2", -1, hn2_copied, 1, 1), ("logits", -1, route, 11, 2)]
        USES += [(f"v{j}", 0, v_spread, 4, j + 1) for j in range(4)]
        USES += [("t1", 1, hn_copied, 1, 1), ("o", 0, o_copied, 1, 1), ("q", 1, q_spread, 4, 4),
                 ("k", 1, k_spread, 4, 4), ("r", 0, ln2, 4, 1)]
        BANK = {use[0]: i % BANKS for i, use in enumerate(USES)}

        def wait_bank(pe, name, i):
            n, at = [use[0] for use in USES].index(name), i
            while True:
                n -= 1
                if n < 0:
                    n, at = n + len(USES), at + -1
                before, offset, semaphore, per, event = USES[n]
                chunk = at + offset
                if BANK[before] == BANK[name] and chunk.exists():
                    return wait(pe, semaphore, chunk.count(per, event))
                if at.static and at.number() < -3:
                    return

        def steps(engine, run):
            for i in range(-1, 4):
                run(Row(0, i, CHUNKS))
            with engine.Fori(2, CHUNKS // 2 - 1) as pair:
                run(Row(pair, 0, CHUNKS))
                run(Row(pair, 1, CHUNKS))
            for i in range(CHUNKS - 2, CHUNKS + 2):
                run(Row(0, i, CHUNKS))

        x1_chunks = x1.rearrange("c s d -> (c s) d").rearrange("(i t p) d -> i p t d", p=128, t=CT)
        out_chunks = out.rearrange("s (i t c) d -> i c s t d", t=CT, c=4)

        block = ctx.enter_context(nc.Block())

        @block.sync
        def _(sp):
            def step(i):
                nxt, m, t = i + 1, i + -1, i + -2
                if nxt.exists():
                    wait(sp, ln1, (nxt + -2).count(3, 3))
                    sp.dma_start(xb[nxt.parity][:, :, :], x1_chunks[nxt.number()]).then_inc(xb_loaded[nxt.parity], 16)
                if m.exists():
                    wait(sp, ln3, (m + -2).count(4, 4))
                    sp.dma_start(xr[m.parity][:, :, :], x1_chunks[m.number()]).then_inc(xr_loaded[m.parity], 16)
                if t.exists():
                    sp.wait_ge(ln3, t.count(4, 4))
                    for c in range(4):
                        sp.dma_start(out_chunks[t.number(), c], fin[t.parity][32 * c:32 * c + 32, :, :]).then_inc(stored[t.parity], 16)

            steps(sp, step)
            for i in range(2):
                sp.wait_ge(stored[i], 64 * (CHUNKS // 2))

        @block.gpsimd
        def _(pool):
            pool.memset(half_neg[:, :], -0.5)
            pool.memset(eps_ct[:, :], EPS)
            pool.memset(e_base[:, :, :], float(np.e)).then_inc(c_made, 1)
            pool.wait_ge(c_made, 2)

            def root(variance, work, done, row, per):
                pool.tensor_tensor(work[:, 0, :], variance, eps_ct[:, :], ALU.add).then_inc(done, 1)
                pool.wait_ge(done, row.count(per, 1))
                pool.tensor_tensor(work[:, 1, :], work[:, 0, :], half_neg[:, :], ALU.pow).then_inc(done, 1)

            def step(i):
                nxt, m, t = i + 1, i + -1, i + -2
                if m.exists():
                    pool.wait_ge(hn2_hi, m.count(1, 1))
                    pool.wait_ge(hn2_copied, m.count(1, 1))
                    wait(pool, up_ready, m.count(16, 0))
                    pool.tensor_tensor(hn2_hl[:, LO, :], hn2T[:, :], hn2_hl[:, HI, :].bitcast(F32), ALU.subtract).then_inc(hn2_lo, 1)
                if m.exists():
                    pool.wait_ge(route, m.count(11, 2))
                    pool.tensor_tensor(r_exp[:, :, :], e_base[:, :, :], l_sub[:, :, :], ALU.pow).then_inc(route_exp, 1)
                if nxt.exists():
                    pool.wait_ge(ln1, nxt.count(3, 2))
                    root(mv1[:, :, 1], root1, ln1_root, nxt, 7)
                    for k, (a, b) in enumerate(((mv1[:, :, 1], root1[:, 1, :]), (root1[:, 2, :], root1[:, 1, :]))):
                        pool.wait_ge(ln1_root, nxt.count(7, k + 2))
                        pool.tensor_tensor(root1[:, k + 2, :], a, b, ALU.mult).then_inc(ln1_root, 1)
                    pool.wait_ge(ln1_root, nxt.count(7, 4))
                    pool.tensor_tensor(root1[:, 4, :], root1[:, 3, :], eps_ct[:, :], ALU.add).then_inc(ln1_root, 1)
                    pool.wait_ge(ln1_root, nxt.count(7, 5))
                    pool.tensor_tensor(root1[:, 5, :], root1[:, 4, :], half_neg[:, :], ALU.pow).then_inc(ln1_root, 1)
                    pool.wait_ge(ln1_root, nxt.count(7, 6))
                    pool.tensor_tensor(root1[:, 6, :], root1[:, 5, :], root1[:, 1, :], ALU.mult).then_inc(ln1_root, 1)
                    pool.wait_ge(ln1, nxt.count(3, 3))
                    pool.tensor_tensor(y0[nxt.parity][:, :, :], y0[nxt.parity][:, :, :],
                                       bo2_sb[:, :].unsqueeze(1).to_broadcast([128, CT, D]), ALU.add).then_inc(y0_biased, 1)
                if t.exists():
                    pool.wait_ge(ln3, t.count(4, 2))
                    root(mv3[:, :, 1], root3, ln3_root, t, 2)
                if i.exists():
                    pool.wait_ge(ln2, i.count(4, 3))
                    root(mv2[:, :, 1], root2, ln2_root, i, 2)

            steps(pool, step)

        @block.scalar
        def _(act):
            for dst, src in ((id_sb[:, :], identity), (m32_f[:, :, :], mask32), (hm_sb[:, :, :], head_masks), (bin_sb[:, :], b_in2),
                             (ln_sb[:, :], ln_cols), (win_sb[:, :], w_in2), (vm_sb[:, :], value_mask), (bo2_sb[:, :], b_out2),
                             (wo2_sb[:, :], w_out2), (router_sb[:, :], router), (tri_sb[:, :, :], tri)):
                act.dma_start(dst, src).then_inc(c_loaded, 16)
            for dst, src in ((w1_sb[:, :, :], w1), (w2_sb[:, :, :, :], w2)):
                act.dma_start(dst, src).then_inc(w_loaded, 16)
            act.wait_ge(c_made, 2)

            def gelu(m, e):
                for half in range(2):
                    act.wait_ge(up_ready, m.count(16, 2 * e + half + 1))
                    if half == 0:
                        wait(act, down_ready, m.count(8, e - 1))
                    act.activation(mid[e % 2][:, half, :], up[half][:, :], ACT.Gelu).then_inc(mid_ready, 1)

            def spread(row, side, heads):
                name, ready, to, done = (("q", q_ready, q_x, q_spread), ("k", k_ready, k_x, k_spread))[side]
                act.wait_ge(ready, row.count(1, 1))
                wait(act, s_ready, row.count(4, 0))
                for n in heads:
                    act.activation(to[:, :, n, :], bank[BANK[name]][:, :].rearrange("p (c s) -> p c s", c=CC),
                                   ACT.Identity, bias=bias_x[:, side, n:n + 1],
                                   scale=hm_sb[:, side, n:n + 1]).then_inc(done, 1)

            def step(i):
                nxt, m = i + 1, i + -1
                for k in range(8):
                    if k == 0 and m.exists():
                        act.wait_ge(t2_ready, m.count(1, 1))
                        wait(act, up_ready, m.count(16, 0))
                        for to, done in ((hn2_hl[:, HI, :], hn2_hi), (hn2T[:, :], hn2_copied)):
                            act.activation(to, bank[BANK["t2"]][:, :], ACT.Identity, bias=ln_sb[:, 3:4],
                                           scale=ln_sb[:, 2:3]).then_inc(done, 1)
                    if k == 6 and i.exists():
                        act.wait_ge(o_ready, i.count(1, 1))
                        wait(act, r_ready, i.count(1, 0))
                        act.activation(oT[:, :], bank[BANK["o"]][:, :], ACT.Identity, bias=bin_sb[:, 2:3]).then_inc(o_copied, 1)
                    if k == 0 and i.exists():
                        act.wait_ge(s_less, i.count(4, 4))
                        wait(act, p_step, i.count(4, 0))
                        act.activation(p_exp[:, :, :, :], s_sub[:, :, :, :], ACT.Exp, scale=HD2 ** -0.5).then_inc(p_ready, 1)
                    if m.exists():
                        gelu(m, k)
                    if k == 5 and nxt.exists():
                        act.wait_ge(t1_ready, nxt.count(1, 1))
                        wait(act, v2_ready, nxt.count(4, 0))
                        act.activation(hnT[:, :], bank[BANK["t1"]][:, :], ACT.Identity, bias=ln_sb[:, 1:2],
                                       scale=ln_sb[:, 0:1]).then_inc(hn_copied, 1)
                    if k >= 5 and nxt.exists():
                        for side, heads in {5: ((0, (0, 1, 2)),), 6: ((0, (3,)), (1, (0, 1, 2))), 7: ((1, (3,)),)}[k]:
                            spread(nxt, side, heads)

            steps(act, step)

        @block.vector
        def _(dve):
            dve.wait_ge(c_loaded, 16 * 11)
            dve.tensor_copy(id_half[:, :], id_sb[:, :])
            dve.tensor_copy(m32_sb[:, :, :], m32_f[:, :, :])
            for side in range(2):
                last = dve.tensor_scalar(bias_x[:, side, :], hm_sb[:, side, :], bin_sb[:, side:side + 1], None, ALU.mult)
            last.then_inc(c_made, 1)
            dve.wait_ge(c_made, 2)
            def split_w1():
                dve.wait_ge(w_loaded, 32)
                dve.tensor_copy(w1_hl[:, HI, :, :], w1_sb[:, :, :]).then_inc(w1_split, 1)
                dve.wait_ge(w1_split, 1)
                dve.tensor_tensor(w1_hl[:, LO, :, :], w1_sb[:, :, :], w1_hl[:, HI, :, :].bitcast(F32), ALU.subtract).then_inc(w1_split, 1)

            def statistics(src, stats, mean_var, done, row, per, first):
                for t in range(CT):
                    last = dve.bn_stats(stats[:, t, :], src[:, t, :])
                last.then_inc(done, 1)
                wait_apart(dve, done, row.count(per, first), spacer[:, :])
                for t in range(CT):
                    last = dve.bn_aggr(mean_var[:, t, :], stats[:, t, :])
                last.then_inc(done, 1)

            def normalise(src, mean_var, root, to):
                for t in range(CT):
                    last = dve.tensor_scalar(to[:, t, :], src[:, t, :], mean_var[:, t, 0:1], root[:, t:t + 1],
                                             ALU.subtract, ALU.mult)
                return last

            def gate(m, e):
                dve.wait_ge(down_ready, m.count(8, e + 1))
                if e == 0:
                    dve.wait_ge(route, m.count(11, 11))
                else:
                    dve.wait_ge(gated, m.count(8, e))
                a = acc[m.parity]
                for t in range(CT):
                    last = dve.scalar_tensor_tensor(out=a[:, t, :], in0=down[e % 2][:, t * D:(t + 1) * D],
                                                    scalar=gates[m.parity][:, t, e:e + 1], in1=a[:, t, :],
                                                    op0=ALU.mult, op1=ALU.add)
                last.then_inc(gated, 1)

            def router_math(m, part):
                steps_done = [2 * part]

                def then(ins):
                    steps_done[0] += 1
                    ins.then_inc(route, 1)
                    dve.wait_ge(route, m.count(11, steps_done[0]))

                logits = bank[BANK["logits"]][:, 0:CT * EXPERTS].rearrange("p (t e) -> p t e", t=CT)
                if part == 0:
                    dve.wait_ge(l_ready, m.count(1, 1))
                    then(dve.tensor_reduce(l_max[:, :], logits, AXIS_X, ALU.max))
                    dve.tensor_tensor(l_sub[:, :, :], logits, l_max[:, :].unsqueeze(2).to_broadcast([128, CT, EXPERTS]),
                                      ALU.subtract).then_inc(route, 1)
                    return
                dve.wait_ge(route_exp, m.count(1, 1))
                then(dve.tensor_reduce(r_sum[:, :], r_exp[:, :, :], AXIS_X, ALU.add))
                then(dve.reciprocal(r_inv[:, :], r_sum[:, :]))
                then(dve.tensor_tensor(r_prob[:, :, :], r_exp[:, :, :], r_inv[:, :].unsqueeze(2).to_broadcast([128, CT, EXPERTS]),
                                       ALU.mult))
                other = r_prob[:, :, :].unsqueeze(2).to_broadcast([128, CT, EXPERTS, EXPERTS])
                own = r_prob[:, :, :].unsqueeze(3).to_broadcast([128, CT, EXPERTS, EXPERTS])
                then(dve.tensor_tensor(above[:, :, :, :], other, own, ALU.is_gt))
                then(dve.tensor_tensor(equal[:, :, :, :], other, own, ALU.is_equal))
                then(dve.tensor_tensor(equal[:, :, :, :], equal[:, :, :, :],
                                       tri_sb[:, :, :].unsqueeze(1).to_broadcast([128, CT, EXPERTS, EXPERTS]), ALU.mult))
                then(dve.tensor_tensor(above[:, :, :, :], above[:, :, :, :], equal[:, :, :, :], ALU.add))
                then(dve.tensor_reduce(rank[:, :, :], above[:, :, :, :], AXIS_X, ALU.add))
                dve.scalar_tensor_tensor(out=gates[m.parity][:, :, :], in0=rank[:, :, :], scalar=float(TOP) - 0.5,
                                         in1=r_prob[:, :, :], op0=ALU.is_lt, op1=ALU.mult).then_inc(route, 1)

            def less_maxima(i):
                wait(dve, p_ready, i.count(1, 0))
                for j in range(4):
                    s = bank[BANK[f"s{j}"]][:, :].rearrange("p (a b) -> p a b", b=ROWS)
                    to = smax[:, 4 * j:4 * j + 4, :].rearrange("p c g -> p (c g)")
                    dve.wait_ge(s_ready, i.count(4, j + 1))
                    dve.tensor_reduce(to, s, AXIS_X, ALU.max).then_inc(s_max, 1)
                    dve.wait_ge(s_max, i.count(4, j + 1))
                    dve.tensor_tensor(s_sub[:, 4 * j:4 * j + 4, :, :].rearrange("p c g t -> p (c g) t"), s,
                                      to.unsqueeze(2).to_broadcast([128, 16, ROWS]), ALU.subtract).then_inc(s_less, 1)

            def step(i):
                nxt, m, t = i + 1, i + -1, i + -2
                for k in range(8):
                    if k == 0:
                        if i.exists():
                            less_maxima(i)
                        if t.exists():
                            gate(t, 7)
                        if m.exists():
                            router_math(m, 0)
                    if k == 0 and nxt.exists():
                        dve.wait_ge(xb_loaded[nxt.parity], nxt.count_of_parity(16, 16))
                        statistics(xb[nxt.parity], st1, mv1, ln1, nxt, 3, 1)
                    if k == 1 and i.exists():
                        dve.wait_ge(p_ready, i.count(1, 1))
                        dve.tensor_reduce(p_sum[:, :, :].rearrange("p c g -> p (c g)"),
                                          p_exp[:, :, :, :].rearrange("p c g t -> p (c g) t"), AXIS_X, ALU.add).then_inc(p_step, 1)
                        dve.wait_ge(p_step, i.count(4, 1))
                        dve.reciprocal(p_inv[:, :, :], p_sum[:, :, :]).then_inc(p_step, 1)
                        dve.wait_ge(p_step, i.count(4, 2))
                        dve.tensor_tensor(p_exp[:, :, :, :].rearrange("p c g t -> p (c g) t"),
                                          p_exp[:, :, :, :].rearrange("p c g t -> p (c g) t"),
                                          p_inv[:, :, :].rearrange("p c g -> p (c g)").unsqueeze(2).to_broadcast([128, CC * 4, ROWS]),
                                          ALU.mult).then_inc(p_step, 1)
                    if k == 1 and m.exists():
                        router_math(m, 1)
                    if k >= 1 and m.exists():
                        gate(m, k - 1)
                    if k == 3 and nxt.exists():
                        dve.wait_ge(ln1_root, nxt.count(7, 7))
                        wait(dve, t1_ready, nxt.count(1, 0))
                        normalise(xb[nxt.parity], mv1, root1[:, 1, :], y0[nxt.parity])
                        normalise(xb[nxt.parity], mv1, root1[:, 6, :], z1).then_inc(ln1, 1)
                        if nxt.static and nxt.number() == 0:
                            split_w1()
                    if k == 3 and i.exists():
                        wait(dve, o_ready, i.count(1, 0))
                        for j in range(4):
                            dve.wait_ge(v2_ready, i.count(4, j + 1))
                            dve.tensor_tensor(v_x[:, 4 * j:4 * j + 4, :], bank[BANK[f"v{j}"]][:, :].rearrange("p (c f) -> p c f", c=4),
                                              vm_sb[:, :].unsqueeze(1).to_broadcast([128, 4, D]), ALU.mult).then_inc(v_spread, 1)
                    if k == 2 and i.exists():
                        dve.wait_ge(p_step, i.count(4, 3))
                        wait(dve, o_ready, i.count(1, 0))
                        dve.transpose(p_T[:, :, :, :].rearrange("p c g t -> p (c g t)"),
                                      p_exp[:, :, :, :].rearrange("p c g t -> p (c g t)")).then_inc(p_step, 1)
                    if k == 4 and t.exists():
                        dve.wait_ge(gated, t.count(8, 8))
                        statistics(acc[t.parity], st3, mv3, ln3, t, 4, 1)
                    if k == 5 and t.exists():
                        dve.wait_ge(ln3_root, t.count(2, 2))
                        wait(dve, stored[t.parity], t.count_of_parity(64, 0))
                        normalise(acc[t.parity], mv3, root3[:, 1, :], fin[t.parity]).then_inc(ln3, 1)
                        dve.wait_ge(ln3, t.count(4, 3))
                        dve.wait_ge(xr_loaded[t.parity], t.count_of_parity(16, 16))
                        dve.tensor_tensor(fin[t.parity][:, :, :], fin[t.parity][:, :, :], xr[t.parity][:, :, :],
                                          ALU.add).then_inc(ln3, 1)
                    if k == 6 and i.exists():
                        dve.wait_ge(r_ready, i.count(1, 1))
                        dve.wait_ge(y0_biased, i.count(1, 1))
                        wait(dve, ln3, (i + -2).count(4, 3))
                        a = acc[i.parity]
                        dve.tensor_tensor(a[:, :, :], bank[BANK["r"]][:, :].rearrange("p (t d) -> p t d", t=CT),
                                          y0[i.parity][:, :, :], ALU.add).then_inc(ln2, 1)
                        dve.wait_ge(ln2, i.count(4, 1))
                        statistics(a, st2, mv2, ln2, i, 4, 2)
                    if k == 7 and i.exists():
                        dve.wait_ge(ln2_root, i.count(2, 2))
                        wait(dve, t2_ready, i.count(1, 0))
                        normalise(acc[i.parity], mv2, root2[:, 1, :], z2).then_inc(ln2, 1)

            steps(dve, step)

        @block.tensor
        def _(pe):
            pe.wait_ge(c_loaded, 16 * 11)
            pe.wait_ge(c_made, 2)

            def first(m, e):
                if e == 0:
                    pe.wait_ge(hn2_hi, m.count(1, 1))
                    if m.static and m.number() == 0:
                        pe.wait_ge(w1_split, 2)
                for half in range(2):
                    wait(pe, mid_ready, m.count(16, 2 * e + half - 1))
                    f = slice(half * 128, half * 128 + 128)
                    pe.matmul(up[half][:, :], w1_hl[:, HI, e, f], hn2_hl[:, HI, :], start=True, stop=False)
                    pe.matmul(up[half][:, :], w1_hl[:, LO, e, f], hn2_hl[:, HI, :], start=False, stop=False)
                    if e == 0 and half == 0:
                        pe.wait_ge(hn2_lo, m.count(1, 1))
                    pe.matmul(up[half][:, :], w1_hl[:, HI, e, f], hn2_hl[:, LO, :],
                              start=False, stop=True).then_inc(up_ready, 1)

            def second(m, e):
                pe.wait_ge(mid_ready, m.count(16, 2 * e + 2))
                wait(pe, gated, m.count(8, e - 1))
                for t in range(CT):
                    for half in range(2):
                        last = pe.matmul(down[e % 2][:, t * D:(t + 1) * D], mid[e % 2][:, half, 128 * t:128 * t + 128],
                                         w2_sb[:, e, half, :], start=half == 0, stop=half == 1)
                last.then_inc(down_ready, 1)

            def transposes(name, src, ready, done, row, i):
                ready()
                wait_bank(pe, name, i)
                for t in range(CT):
                    last = pe.transpose(bank[BANK[name]][:, t * 128:(t + 1) * 128], src[:, t, :], id_sb[:, :])
                last.then_inc(done, 1)

            def step(i):
                nxt, m, t = i + 1, i + -1, i + -2
                for k in range(8):
                    if k == 0:
                        if i.exists():
                            pe.wait_ge(q_spread, i.count(4, 4))
                            pe.wait_ge(k_spread, i.count(4, 4))
                            for j in range(4):
                                wait_bank(pe, f"s{j}", i)
                                b = bank[BANK[f"s{j}"]]
                                pe.matmul(b[:, :], id_half[:, :], m32_sb[:, :, :], start=True, stop=False, skip_group_check=True)
                                for n in range(4):
                                    c = 4 * j + n
                                    last = pe.matmul(b[:, n * 128:(n + 1) * 128], q_x[:, c, :, :], k_x[:, c, :, :],
                                                     start=False, stop=True, skip_group_check=True)
                                last.then_inc(s_ready, 1)
                        if m.exists():
                            transposes("t2", z2, lambda: pe.wait_ge(ln2, m.count(4, 4)), t2_ready, m, i)
                        if t.exists():
                            second(t, 7)
                        if m.exists():
                            pe.wait_ge(hn2_copied, m.count(1, 1))
                            wait_bank(pe, "logits", i)
                            for n in range(CT):
                                last = pe.matmul(bank[BANK["logits"]][:, n * EXPERTS:(n + 1) * EXPERTS],
                                                 hn2T[:, 128 * n:128 * n + 128], router_sb[:, :], start=True, stop=True)
                            last.then_inc(l_ready, 1)
                    if m.exists():
                        first(m, k)
                    if k == 0 and i.exists():
                        for j in range(4):
                            wait_bank(pe, f"v{j}", i)
                            for n in range(4):
                                tokens = ROWS * (4 * j + n)
                                for g in range(4):
                                    last = pe.matmul(bank[BANK[f"v{j}"]][32 * g:32 * g + 32, n * D:(n + 1) * D],
                                                     hnT[:, tokens:tokens + ROWS], win_sb[:, 2 * D:3 * D],
                                                     start=True, stop=True)
                            last.then_inc(v2_ready, 1)
                    if k >= 1 and m.exists():
                        second(m, k - 1)
                    if k == 5 and nxt.exists():
                        transposes("t1", z1, lambda: pe.wait_ge(ln1, nxt.count(3, 3)), t1_ready, nxt, i)
                    if k == 5 and i.exists():
                        pe.wait_ge(p_step, i.count(4, 4))
                        pe.wait_ge(v_spread, i.count(4, 4))
                        for c in range(CC):
                            for g in range(4):
                                last = pe.matmul(bank[BANK["o"]][32 * g:32 * g + 32, ROWS * c:ROWS * c + ROWS],
                                                 v_x[:, c, 32 * g:32 * g + 32], p_T[:, c, g, :], start=True, stop=True)
                        last.then_inc(o_ready, 1)
                    if k == 5 and nxt.exists():
                        pe.wait_ge(hn_copied, nxt.count(1, 1))
                        for side, (name, ready) in enumerate((("q", q_ready), ("k", k_ready))):
                            wait_bank(pe, name, i)
                            pe.matmul(bank[BANK[name]][:, :], win_sb[:, side * D:(side + 1) * D], hnT[:, :],
                                      start=True, stop=True).then_inc(ready, 1)
                    if k == 6 and i.exists():
                        pe.wait_ge(o_copied, i.count(1, 1))
                        wait_bank(pe, "r", i)
                        for n in range(CT):
                            last = pe.matmul(bank[BANK["r"]][:, n * D:(n + 1) * D], oT[:, 128 * n:128 * n + 128], wo2_sb[:, :],
                                             start=True, stop=True)
                        last.then_inc(r_ready, 1)

            steps(pe, step)


def build(nc, ins, out):
    x1 = nc.dram_tensor("x1", (COLS, ROWS, D), F32, kind="Internal").ap()
    attention_part(nc, ins["x"].rearrange("b (t p) d -> b p t d", p=128), ins["w_qkv"], ins["w_out"], ins["bias_qk"],
                   ins["bias_v"], ins["bias_out"], ins["turns"], ins["identity"], ins["masks"],
                   x1.rearrange("(t p) b d -> b p t d", p=128))
    names = ["w_in2", "b_in2", "w_out2", "b_out2", "ln_cols", "router", "w1", "w2", "identity", "head_masks",
             "value_mask", "mask32", "tri"]
    second_part(nc, x1, out, *[ins[n] for n in names])


def host_layouts(inputs):
    f = {k: np.asarray(v) for k, v in inputs.items()}
    w = f["L0_attn_W_in"]
    qk = w[:2 * FEATS].reshape(2, QUADS, 4, 2, HALF, D).transpose(5, 0, 1, 3, 2, 4).reshape(D, 2 * FEATS)
    b = f["L0_attn_b_in"]
    p = np.arange(HALF, dtype=np.float32) / np.float32(HALF - 1)
    thetas = np.float32(MIN_THETA) * np.float32(MAX_THETA / MIN_THETA) ** p
    angle = np.arange(COLS, dtype=np.float32)[None, :] / thetas[:, None]
    sin, cos = (np.tile(t(angle), (4, 1)).astype(np.float32) for t in (np.sin, np.cos))
    hidden = np.where(np.arange(128)[None, :] > np.arange(128)[:, None], np.float32(MASKED), np.float32(0))
    part = np.arange(128)

    def one_if(test):
        return test.astype(np.float32)

    return {
        "x": f["L0_attn_x"],
        "w_qkv": np.concatenate([qk, w[2 * FEATS:].T], axis=1),
        "w_out": f["L0_attn_W_out"].T.reshape(PAIRS, 128, D).transpose(1, 0, 2),
        "bias_qk": b[:2 * FEATS].reshape(2, QUADS, 4, 2, HALF).transpose(2, 4, 0, 1, 3).reshape(128, -1),
        "bias_v": b[2 * FEATS:].reshape(PAIRS, 128).T,
        "bias_out": f["L0_attn_b_out"][None, :],
        "turns": np.stack([np.stack([sin, cos], 1), np.stack([cos, -sin], 1)], 1),
        "identity": np.eye(128, dtype=np.float32),
        "w_in2": f["L0_ffn_in_proj_w"].T,
        "b_in2": f["L0_ffn_in_proj_b"].reshape(3, D).T,
        "w_out2": f["L0_ffn_out_proj_w"].T,
        "b_out2": np.tile(f["L0_ffn_out_proj_b"], (128, 1)),
        "ln_cols": np.stack([f["L0_ffn_" + n] for n in ("ln1_w", "ln1_b", "ln2_w", "ln2_b")], 1),
        "router": f["L0_ffn_router_w"].T,
        "w1": f["L0_ffn_w1"].transpose(1, 0, 2),
        "w2": f["L0_ffn_w2"].reshape(EXPERTS, 2, 128, D).transpose(2, 0, 1, 3),
        "head_masks": one_if(np.stack([(part % 32 // HD2)[:, None] == np.arange(4), (part // 32)[:, None] == np.arange(4)], 1)),
        "value_mask": one_if((part // 32)[:, None] == (np.arange(D) % 32 // HD2)[None, :]),
        "mask32": np.tile(np.where(np.arange(ROWS)[None, :] > (part % ROWS)[:, None], np.float32(MASKED), np.float32(0))[:, None, :], (1, 16, 1)),
        "tri": np.tile(one_if(np.arange(EXPERTS)[None, :] < np.arange(EXPERTS)[:, None]), (128, 1, 1)),
        "masks": np.stack([np.stack([hidden] * 2, 1), np.stack([hidden.T] * 2, 1)], 1),
    }


def kernel(**inputs):
    import concourse.bacc as _bacc
    from concourse.bass_utils import run_bass_kernel_spmd as _run

    nc = _bacc.Bacc("TRN2", target_bir_lowering=False, num_devices=1)
    arrays, ins = {}, {}
    for name, a in host_layouts(inputs).items():
        arrays[f"in_{name}"] = np.ascontiguousarray(a)
        ins[name] = nc.dram_tensor(f"in_{name}", a.shape, F32, kind="ExternalInput").ap()
    out = nc.dram_tensor("out", (ROWS, COLS, D), F32, kind="ExternalOutput").ap()
    build(nc, ins, out)
    return _run(nc, [arrays], core_ids=[0]).results[0]["out"]
```
